# Optimizing a Trainium2 kernel written in Bass

```python
import numpy as np
import jax
import jax.numpy as jnp

def _softmax(x, axis=-1):
    return jax.nn.softmax(x, axis=axis)

def _gelu(x):
    return jax.nn.gelu(x, approximate=True)

def _silu(x):
    return jax.nn.silu(x)

def _sigmoid(x):
    return jax.nn.sigmoid(x)

def _layernorm(x, axis=-1, eps=1e-05):
    m = jnp.mean(x, axis=axis, keepdims=True)
    v = jnp.var(x, axis=axis, keepdims=True)
    return (x - m) / jnp.sqrt(v + eps)

def _scatter_add(tgt, idx, src, axis=0):
    return tgt.at[idx].add(src)

def _segment_sum(src, seg, n):
    return jax.ops.segment_sum(src, seg, n)
kernel_name = 'mk_decoder_postln_d1_seqx_r4_7f59ad'

def setup_inputs(seed: int=0):
    np.random.seed(seed)
    _w = jnp.asarray

    def _rec_inputs():
        import jax
        import jax.numpy as jnp
        _rk = jax.random.key(seed)
        x = -0.0002928 + 1 * jax.random.normal(jax.random.fold_in(_rk, 1), (1, 2048, 256), jnp.float32)
        _lenS = 2048 - jax.random.randint(jax.random.fold_in(_rk, 7), (1,), 0, max(1, 2048 // 4) + 1, jnp.int32)
        _lenS2 = 1601 - jax.random.randint(jax.random.fold_in(_rk, 8), (1,), 0, max(1, 1601 // 4) + 1, jnp.int32)
        _ctx_1024P = jax.random.normal(jax.random.fold_in(_rk, 11), (1, 16, 256), jnp.float32)
        _ctx_1024c = jax.random.dirichlet(jax.random.fold_in(_rk, 511), 0.3 * jnp.ones((16,), jnp.float32), (1, 1601))
        _ctx_1024t = jnp.einsum('bsk,bkd->bsd', _ctx_1024c, _ctx_1024P)
        _ctx_1024t = _ctx_1024t * jax.lax.rsqrt(jnp.mean(jnp.square(_ctx_1024t)) + 1e-12) * 0.953939
        ctx_1024 = 4.13588e-05 + 0.999923 * (_ctx_1024t + 0.3 * jax.random.normal(jax.random.fold_in(_rk, 611), (1, 1601, 256), jnp.float32))
        itok_BxS_8_8191 = jax.random.randint(jax.random.fold_in(_rk, 12), (1, 2048), 8, 2048, jnp.int32)
        itok_BxS2_1_8191 = jax.random.randint(jax.random.fold_in(_rk, 13), (1, 1601), 1, 2048, jnp.int32)
        _validS = jnp.arange(2048)[None, :] < _lenS[:, None]
        _validS2 = jnp.arange(1601)[None, :] < _lenS2[:, None]
        _causal = jnp.tril(jnp.ones((2048, 2048), dtype=bool))
        mask_BxSxS2_if1 = jnp.where(jnp.ones((1, 2048, 1601), dtype=bool), 1, 0).astype(jnp.int32)
        return (x, ctx_1024, itok_BxS_8_8191, itok_BxS2_1_8191, mask_BxSxS2_if1)
    x, ctx_1024, itok_BxS_8_8191, itok_BxS2_1_8191, mask_BxSxS2_if1 = _rec_inputs()

    def _L0_attn_setup():
        import jax, jax.numpy as jnp
        import numpy as np
        D_MODEL = 256
        D_STATE = 16
        D_CONV = 4
        EXPAND = 2
        INNER = EXPAND * D_MODEL
        DT_RANK = (D_MODEL + 15) // 16
        BATCH = 1
        SEQLEN = 512
        DT_MIN, DT_MAX, DT_FLOOR = (0.001, 0.1, 0.0001)

        def _silu(x):
            return x * jax.nn.sigmoid(x)
        key = jax.random.key(seed)
        ks = jax.random.split(key, 8)
        hidden_states = jax.random.normal(ks[0], (BATCH, SEQLEN, D_MODEL), jnp.float32)
        W_in = jax.random.normal(ks[1], (2 * INNER, D_MODEL), jnp.float32) * D_MODEL ** (-0.5)
        conv_w = jax.random.normal(ks[2], (INNER, D_CONV), jnp.float32) * 0.02
        conv_b = jnp.zeros((INNER,), jnp.float32)
        W_x = jax.random.normal(ks[3], (DT_RANK + 2 * D_STATE, INNER), jnp.float32) * INNER ** (-0.5)
        dt_init_std = DT_RANK ** (-0.5)
        W_dt = jax.random.uniform(ks[4], (INNER, DT_RANK), jnp.float32, -dt_init_std, dt_init_std)
        dt = jnp.exp(jax.random.uniform(ks[5], (INNER,), jnp.float32) * (np.log(DT_MAX) - np.log(DT_MIN)) + np.log(DT_MIN))
        dt = jnp.clip(dt, DT_FLOOR)
        dt_bias = dt + jnp.log(-jnp.expm1(-dt))
        A_log = jax.random.normal(ks[6], (INNER, D_STATE), jnp.float32) * 0.5
        D_skip = jnp.ones((INNER,), jnp.float32)
        W_out = jax.random.normal(ks[7], (D_MODEL, INNER), jnp.float32) * INNER ** (-0.5)
        return dict(hidden_states=hidden_states, W_in=W_in, conv_w=conv_w, conv_b=conv_b, W_x=W_x, W_dt=W_dt, dt_bias=dt_bias, A_log=A_log, D_skip=D_skip, W_out=W_out)
    _L0_attn_all = _L0_attn_setup()
    _L0_attn_in = {k: v for k, v in _L0_attn_all.items() if k in ('W_in', 'conv_w', 'conv_b', 'W_x', 'W_dt', 'dt_bias', 'A_log', 'D_skip', 'W_out')}
    del _L0_attn_all

    def _L0_xattn_setup():
        import jax, jax.numpy as jnp
        import numpy as np
        DIM = 256
        NUM_HEADS = 16
        HEAD_DIM = DIM // NUM_HEADS

        def _slopes(num_heads):
            ratio = 2.0 ** (-8.0 / num_heads)
            return jnp.asarray([ratio ** i for i in range(1, num_heads + 1)], dtype=jnp.float32)
        key = jax.random.key(seed)
        ks = jax.random.split(key, 10)
        b, q_len, k_len = (2, 512, 1024)
        query = jax.random.normal(ks[0], (b, q_len, DIM), dtype=jnp.float32)
        keys = jax.random.normal(ks[1], (b, k_len, DIM), dtype=jnp.float32)
        values = jax.random.normal(ks[2], (b, k_len, DIM), dtype=jnp.float32)
        query_pos = jnp.sort(jax.random.randint(ks[3], (b, q_len), 0, 2048), axis=-1)
        key_pos = jnp.sort(jax.random.randint(ks[4], (b, k_len), 0, 2048), axis=-1)
        mask = jnp.ones((b, q_len, k_len), dtype=jnp.int32)
        lim = float(np.sqrt(6.0 / (DIM + DIM)))
        W_q = jax.random.uniform(ks[5], (DIM, DIM), minval=-lim, maxval=lim, dtype=jnp.float32)
        W_k = jax.random.uniform(ks[6], (DIM, DIM), minval=-lim, maxval=lim, dtype=jnp.float32)
        W_v = jax.random.uniform(ks[7], (DIM, DIM), minval=-lim, maxval=lim, dtype=jnp.float32)
        W_o = jax.random.uniform(ks[8], (DIM, DIM), minval=-lim, maxval=lim, dtype=jnp.float32)
        return {'query': query, 'keys': keys, 'values': values, 'W_q': W_q, 'W_k': W_k, 'W_v': W_v, 'W_o': W_o, 'query_pos': query_pos, 'key_pos': key_pos, 'mask': mask}
    _L0_xattn_all = _L0_xattn_setup()
    _L0_xattn_in = {k: v for k, v in _L0_xattn_all.items() if k in ('W_q', 'W_k', 'W_v', 'W_o')}
    del _L0_xattn_all

    def _L0_ffn_setup():
        import jax, jax.numpy as jnp
        import numpy as np
        from jax import lax
        T, B, I, M, O = (64, 64, 256, 256, 256)

        def _xavier(key, shape):
            fan_out, fan_in = shape
            limit = float(np.sqrt(6.0 / (fan_in + fan_out)))
            return jax.random.uniform(key, shape, jnp.float32, -limit, limit)
        key = jax.random.key(seed)
        ks = jax.random.split(key, 9)
        x = jax.random.normal(ks[0], (T, B, I), jnp.float32)
        return {'x': x, 'wf': _xavier(ks[1], (M, I)), 'uf': _xavier(ks[2], (M, M)), 'bf': jnp.zeros((M,), jnp.float32), 'wi': _xavier(ks[3], (M, I)), 'ui': _xavier(ks[4], (M, M)), 'bi': jnp.zeros((M,), jnp.float32), 'wc': _xavier(ks[5], (M, I)), 'uc': _xavier(ks[6], (M, M)), 'bc': jnp.zeros((M,), jnp.float32), 'wo': _xavier(ks[7], (O, I)), 'uo': _xavier(ks[8], (O, M)), 'bo': jnp.zeros((O,), jnp.float32), 'in_c': jnp.zeros((M,), jnp.float32)}
    _L0_ffn_all = _L0_ffn_setup()
    _L0_ffn_in = {k: v for k, v in _L0_ffn_all.items() if k in ('wf', 'uf', 'bf', 'wi', 'ui', 'bi', 'wc', 'uc', 'bc', 'wo', 'uo', 'bo', 'in_c')}
    del _L0_ffn_all
    return {'x': x, 'ctx_1024': ctx_1024, 'itok_BxS_8_8191': itok_BxS_8_8191, 'itok_BxS2_1_8191': itok_BxS2_1_8191, 'mask_BxSxS2_if1': mask_BxSxS2_if1, 'L0_attn_W_in': _L0_attn_in['W_in'], 'L0_attn_conv_w': _L0_attn_in['conv_w'], 'L0_attn_conv_b': _L0_attn_in['conv_b'], 'L0_attn_W_x': _L0_attn_in['W_x'], 'L0_attn_W_dt': _L0_attn_in['W_dt'], 'L0_attn_dt_bias': _L0_attn_in['dt_bias'], 'L0_attn_A_log': _L0_attn_in['A_log'], 'L0_attn_D_skip': _L0_attn_in['D_skip'], 'L0_attn_W_out': _L0_attn_in['W_out'], 'L0_xattn_W_q': _L0_xattn_in['W_q'], 'L0_xattn_W_k': _L0_xattn_in['W_k'], 'L0_xattn_W_v': _L0_xattn_in['W_v'], 'L0_xattn_W_o': _L0_xattn_in['W_o'], 'L0_ffn_wf': _L0_ffn_in['wf'], 'L0_ffn_uf': _L0_ffn_in['uf'], 'L0_ffn_bf': _L0_ffn_in['bf'], 'L0_ffn_wi': _L0_ffn_in['wi'], 'L0_ffn_ui': _L0_ffn_in['ui'], 'L0_ffn_bi': _L0_ffn_in['bi'], 'L0_ffn_wc': _L0_ffn_in['wc'], 'L0_ffn_uc': _L0_ffn_in['uc'], 'L0_ffn_bc': _L0_ffn_in['bc'], 'L0_ffn_wo': _L0_ffn_in['wo'], 'L0_ffn_uo': _L0_ffn_in['uo'], 'L0_ffn_bo': _L0_ffn_in['bo'], 'L0_ffn_in_c': _L0_ffn_in['in_c']}

def reference(x, ctx_1024, itok_BxS_8_8191, itok_BxS2_1_8191, mask_BxSxS2_if1, L0_attn_W_in, L0_attn_conv_w, L0_attn_conv_b, L0_attn_W_x, L0_attn_W_dt, L0_attn_dt_bias, L0_attn_A_log, L0_attn_D_skip, L0_attn_W_out, L0_xattn_W_q, L0_xattn_W_k, L0_xattn_W_v, L0_xattn_W_o, L0_ffn_wf, L0_ffn_uf, L0_ffn_bf, L0_ffn_wi, L0_ffn_ui, L0_ffn_bi, L0_ffn_wc, L0_ffn_uc, L0_ffn_bc, L0_ffn_wo, L0_ffn_uo, L0_ffn_bo, L0_ffn_in_c):
    import jax
    import jax.numpy as jnp

    def _L0_attn_ref(hidden_states, W_in, conv_w, conv_b, W_x, W_dt, dt_bias, A_log, D_skip, W_out):
        import jax, jax.numpy as jnp
        import numpy as np
        D_MODEL = 256
        D_STATE = 16
        D_CONV = 4
        EXPAND = 2
        INNER = EXPAND * D_MODEL
        DT_RANK = (D_MODEL + 15) // 16
        BATCH = 1
        SEQLEN = 512
        DT_MIN, DT_MAX, DT_FLOOR = (0.001, 0.1, 0.0001)

        def _silu(x):
            return x * jax.nn.sigmoid(x)
        xz = hidden_states @ W_in.T
        proj, gate = jnp.split(xz, 2, axis=-1)
        xc = proj.transpose(0, 2, 1)
        kernel = conv_w[:, None, :]
        conv = jax.lax.conv_general_dilated(xc, kernel, window_strides=(1,), padding=[(D_CONV - 1, 0)], dimension_numbers=('NCH', 'OIH', 'NCH'), feature_group_count=INNER)
        conv = _silu(conv + conv_b[None, :, None])
        u = conv.transpose(0, 2, 1)
        projt = u @ W_x.T
        dt_lr, Bp, Cp = jnp.split(projt, [DT_RANK, DT_RANK + D_STATE], axis=-1)
        delta = jax.nn.softplus(dt_lr @ W_dt.T + dt_bias)
        A = -jnp.exp(A_log)
        dA = jnp.exp(jnp.einsum('bld,dn->lbdn', delta, A))
        dBu = jnp.einsum('bld,bln,bld->lbdn', delta, Bp, u)

        def step(h, inp):
            dA_t, dBu_t = inp
            h = dA_t * h + dBu_t
            return (h, h)
        h0 = jnp.zeros((hidden_states.shape[0], INNER, D_STATE), u.dtype)
        _, hs = jax.lax.scan(step, h0, (dA, dBu))
        y = jnp.einsum('lbdn,bln->bld', hs, Cp)
        y = y + D_skip * u
        y = y * _silu(gate)
        return y @ W_out.T

    def _L0_xattn_ref(query, keys, values, W_q, W_k, W_v, W_o, query_pos, key_pos, mask):
        import jax, jax.numpy as jnp
        import numpy as np
        DIM = 256
        NUM_HEADS = 16
        HEAD_DIM = DIM // NUM_HEADS

        def _slopes(num_heads):
            ratio = 2.0 ** (-8.0 / num_heads)
            return jnp.asarray([ratio ** i for i in range(1, num_heads + 1)], dtype=jnp.float32)
        b, q_len, _ = query.shape
        k_len = keys.shape[1]
        scale = 1.0 / np.sqrt(HEAD_DIM)
        Q = (query @ W_q.T).reshape(b, q_len, NUM_HEADS, HEAD_DIM).transpose(0, 2, 1, 3)
        K = (keys @ W_k.T).reshape(b, k_len, NUM_HEADS, HEAD_DIM).transpose(0, 2, 1, 3)
        V = (values @ W_v.T).reshape(b, k_len, NUM_HEADS, HEAD_DIM).transpose(0, 2, 1, 3)
        scores = jnp.einsum('bhqd,bhkd->bhqk', Q, K) * scale
        dist = (query_pos[:, :, None] - key_pos[:, None, :]).astype(scores.dtype)
        bias = -_slopes(NUM_HEADS)[None, :, None, None] * dist[:, None, :, :]
        scores = scores + bias
        scores = jnp.where(mask[:, None, :, :] == 0, -jnp.inf, scores)
        m = jnp.max(scores, axis=-1, keepdims=True)
        e = jnp.exp(scores - m)
        attn = e / (1.0 + jnp.sum(e, axis=-1, keepdims=True))
        out = jnp.einsum('bhqk,bhkd->bhqd', attn, V)
        out = out.transpose(0, 2, 1, 3).reshape(b, q_len, DIM)
        return out @ W_o.T

    def _L0_ffn_ref(x, wf, uf, bf, wi, ui, bi, wc, uc, bc, wo, uo, bo, in_c):
        import jax, jax.numpy as jnp
        import numpy as np
        from jax import lax
        T, B, I, M, O = (64, 64, 256, 256, 256)

        def _xavier(key, shape):
            fan_out, fan_in = shape
            limit = float(np.sqrt(6.0 / (fan_in + fan_out)))
            return jax.random.uniform(key, shape, jnp.float32, -limit, limit)
        batch = x.shape[1]
        c0 = jnp.broadcast_to(in_c, (batch, in_c.shape[0]))

        def step(c, xt):
            ft = jax.nn.sigmoid(xt @ wf.T + c @ uf.T + bf)
            it = jax.nn.sigmoid(xt @ wi.T + c @ ui.T + bi)
            gt = jnp.tanh(xt @ wc.T + c @ uc.T + bc)
            c = ft * c + it * gt
            return (c, None)
        c_final, _ = lax.scan(step, c0, x)
        h = jnp.tanh(jnp.einsum('tbi,oi->tbo', x, wo) + c_final @ uo.T + bo)
        return h
    x = _layernorm(x + _L0_attn_ref(x, L0_attn_W_in, L0_attn_conv_w, L0_attn_conv_b, L0_attn_W_x, L0_attn_W_dt, L0_attn_dt_bias, L0_attn_A_log, L0_attn_D_skip, L0_attn_W_out), axis=-1)
    x = _layernorm(x + _L0_xattn_ref(x, ctx_1024, ctx_1024, L0_xattn_W_q, L0_xattn_W_k, L0_xattn_W_v, L0_xattn_W_o, itok_BxS_8_8191, itok_BxS2_1_8191, mask_BxSxS2_if1), axis=-1)
    x = _layernorm(x + _L0_ffn_ref(x, L0_ffn_wf, L0_ffn_uf, L0_ffn_bf, L0_ffn_wi, L0_ffn_ui, L0_ffn_bi, L0_ffn_wc, L0_ffn_uc, L0_ffn_bc, L0_ffn_wo, L0_ffn_uo, L0_ffn_bo, L0_ffn_in_c), axis=-1)
    return x

_drawn_inputs = setup_inputs


def setup_inputs(seed=0):
    import zlib

    import numpy as np

    out = dict(_drawn_inputs(seed))
    spreads = {'L0_attn_conv_b': (0.0, 0.1),
     'L0_attn_D_skip': (1.0, 0.6),
     'L0_ffn_bf': (0.0, 2.0),
     'L0_ffn_bi': (0.0, 0.8),
     'L0_ffn_bc': (0.0, 0.414),
     'L0_ffn_bo': (0.0, 0.1),
     'L0_ffn_in_c': (0.0, 0.1)}
    factors = {'L0_attn_conv_w': 3.863,
     'L0_attn_W_x': 8.0,
     'L0_attn_W_dt': 8.0,
     'L0_attn_dt_bias': 8.0,
     'L0_attn_A_log': 8.0,
     'L0_ffn_wf': 15.869,
     'L0_ffn_uf': 185.811,
     'L0_ffn_ui': 7.581,
     'L0_ffn_uc': 3.114}
    for name, (base, spread) in spreads.items():
        noise = np.random.default_rng([zlib.crc32(name.encode()), seed]).standard_normal(out[name].shape)
        drawn = base * np.exp(spread * noise) if base else spread * noise
        out[name] = jnp.asarray(drawn.astype(out[name].dtype))
    for name, factor in factors.items():
        out[name] = (out[name] * factor).astype(out[name].dtype)
    return out
```

```python
import concourse.bass as bass
from concourse import mybir
from contextlib import ExitStack

F32 = mybir.dt.float32
BF16 = mybir.dt.bfloat16
I32 = mybir.dt.int32
ALU = mybir.AluOpType
ACT = mybir.ActivationFunctionType
AX = mybir.AxisListType

P = 128
L = 2048
D = 256
DI = 512
NS = 16
R = 16
TAPS = 4
S2 = 1601
H = 16
HD = D // H
CH = 512
NC = L // CH
LT = CH // P
DB = DI // P
DK = D // P
KT = (S2 + P - 1) // P
KLAST = S2 - (KT - 1) * P
HG = 4
G = H // HG
EPS = 1e-5
QPART = (0, 0, 1, 1, 0, 2)
KPART = (0, 1, 0, 1, 2, 0)
NPAIR = len(QPART)
ROWS_A = NPAIR * HD + 3
ROWS_B = ROWS_A + 3
ONES0 = NPAIR * HD
MW = 401
MSTEP = 400
MASKED = 2.0 ** 100


def wait_alone(eng, sem, value, passed):
    eng.wait_ge(sem, value)
    eng.sem_inc(passed, 1)


def keys_values(nc, io, keep, scratch):
    with ExitStack() as ctx:
        sb = lambda n, s, t=F32: ctx.enter_context(nc.sbuf_tensor(n, s, t))
        sem = lambda n: ctx.enter_context(nc.semaphore(n))
        ps = [ctx.enter_context(nc.psum_tensor(f"kv_ps{i}", [P, 512], F32)) for i in range(8)]
        ctxT = sb("ctxT", [P, DK, S2])
        wk = sb("wk", [P, DK, D])
        wv = sb("wv", [P, DK, D])
        kpart = sb("kpart", [P, DK, 3, S2], BF16)
        krest = sb("krest", [P, DK, S2])
        pos = sb("pos", [H, S2], I32)
        posf = sb("posf", [H, S2])
        kb = sb("kb", [H, S2])
        kbrest = sb("kbrest", [H, S2])
        kbpart = sb("kbpart", [H, 3, S2], BF16)
        slopes = sb("slopes", [H, 1])
        pmax = sb("pmax", [H, 1])
        loaded, pos_loaded = sem("kv_loaded"), sem("pos_loaded")
        k_done, v_done, k1_done, r_done, k2_done, k3_done = (sem(n) for n in (
            "k_done", "v_done", "k1_done", "krest_done", "k2_done", "k3_done"))
        v_out, v1_set, bias_step, stored = sem("v_out"), sem("v1_set"), sem("bias_step"), sem("kv_stored")
        V1 = keep["V1"]
        cuts = [(n * 512, min(512, S2 - n * 512)) for n in range(4)]
        units = [(m, n) for n in range(4) for m in range(DK)]

        with nc.Block() as block:
            @block.sync
            def _(sp):
                sp.dma_start(ctxT[:], io["ctxT"].rearrange("(k p) n -> p k n", p=P)).then_inc(loaded, 16)
                sp.dma_start(wk[:], io["WkT"].rearrange("(k p) n -> p k n", p=P)).then_inc(loaded, 16)
                sp.dma_start(wv[:], io["WvT"].rearrange("(k p) n -> p k n", p=P)).then_inc(loaded, 16)
                sp.dma_start(pos[:], io["kpos"].broadcast_to([H, S2])).then_inc(pos_loaded, 16)
                sp.dma_start(slopes[:], io["slopes"]).then_inc(pos_loaded, 16)
                sp.dma_start(keep["ident"][:], io["ident"]).then_inc(pos_loaded, 16)
                sp.wait_ge(k3_done, len(units))
                for m in range(DK):
                    sp.dma_start(scratch["kd"][:, m * P:(m + 1) * P, :].rearrange("j p n -> p j n"),
                                 kpart[:, m, :, :]).then_inc(stored, 16)
                sp.wait_ge(bias_step, 7)
                sp.dma_start(scratch["kbd"].rearrange("j h n -> h j n"), kbpart[:]).then_inc(stored, 16)
                sp.wait_ge(stored, 48)
                sp.wait_ge(pos_loaded, 48)

            @block.gpsimd
            def _(pool):
                pool.memset(V1[:, :, :, HD:], 0.0).then_inc(v1_set, 1)
                pool.wait_ge(v1_set, 1)
                pool.memset(V1[:, :, :, HD:HD + 1], 1.0).then_inc(v1_set, 1)

            @block.tensor
            def _(pe):
                pe.wait_ge(loaded, 48)
                for u, (m, n) in enumerate(units):
                    lo, w = cuts[n]
                    for k in range(DK):
                        mm = pe.matmul(ps[u][:, 0:w], wk[:, k, m * P:(m + 1) * P], ctxT[:, k, lo:lo + w],
                                       start=(k == 0), stop=(k == DK - 1))
                    mm.then_inc(k_done, 1)
                for t in range(KT):
                    rows = P if t < KT - 1 else KLAST
                    if t < 8:
                        pe.wait_ge(r_done, t + 1)
                    else:
                        pe.wait_ge(v_out, t - 7)
                    for k in range(DK):
                        mm = pe.matmul(ps[t % 8][0:rows, 0:D], ctxT[:, k, t * P:t * P + rows], wv[:, k, :],
                                       start=(k == 0), stop=(k == DK - 1))
                    mm.then_inc(v_done, 1)

            def second(act, u):
                m, n = units[u]
                lo, w = cuts[n]
                act.wait_ge(r_done, u + 1)
                act.copy(kpart[:, m, 1, lo:lo + w], krest[:, m, lo:lo + w]).then_inc(k2_done, 1)

            @block.scalar
            def _(act):
                for u, (m, n) in enumerate(units):
                    lo, w = cuts[n]
                    act.wait_ge(k_done, u + 1)
                    act.copy(kpart[:, m, 0, lo:lo + w], ps[u][:, 0:w]).then_inc(k1_done, 1)
                    if u:
                        second(act, u - 1)
                second(act, len(units) - 1)
                for t in range(KT):
                    rows = P if t < KT - 1 else KLAST
                    act.wait_ge(v_done, t + 1)
                    act.copy(V1[0:rows, t, :, 0:HD],
                             ps[t % 8][0:rows, 0:D].rearrange("p (h e) -> p h e", h=H)).then_inc(v_out, 1)

            @block.vector
            def _(dve):
                for u, (m, n) in enumerate(units):
                    lo, w = cuts[n]
                    dve.wait_ge(k1_done, u + 1)
                    dve.tensor_tensor(krest[:, m, lo:lo + w], ps[u][:, 0:w], kpart[:, m, 0, lo:lo + w],
                                      ALU.subtract).then_inc(r_done, 1)
                for u, (m, n) in enumerate(units):
                    lo, w = cuts[n]
                    dve.wait_ge(k2_done, u + 1)
                    dve.tensor_tensor(kpart[:, m, 2, lo:lo + w], krest[:, m, lo:lo + w],
                                      kpart[:, m, 1, lo:lo + w], ALU.subtract).then_inc(k3_done, 1)
                dve.wait_ge(pos_loaded, 48)
                dve.tensor_copy(posf[:], pos[:]).then_inc(bias_step, 1)
                dve.wait_ge(bias_step, 1)
                dve.tensor_reduce(pmax[:], posf[:], AX.X, ALU.max).then_inc(bias_step, 1)
                dve.wait_ge(bias_step, 2)
                dve.tensor_scalar(kb[:], posf[:], pmax[:], slopes[:], ALU.subtract, ALU.mult).then_inc(bias_step, 1)
                dve.wait_ge(bias_step, 3)
                dve.tensor_copy(kbpart[:, 0, :], kb[:]).then_inc(bias_step, 1)
                dve.wait_ge(bias_step, 4)
                dve.tensor_tensor(kbrest[:], kb[:], kbpart[:, 0, :], ALU.subtract).then_inc(bias_step, 1)
                dve.wait_ge(bias_step, 5)
                dve.tensor_copy(kbpart[:, 1, :], kbrest[:]).then_inc(bias_step, 1)
                dve.wait_ge(bias_step, 6)
                dve.tensor_tensor(kbpart[:, 2, :], kbrest[:], kbpart[:, 1, :], ALU.subtract).then_inc(bias_step, 1)


def ssm_inputs(nc, io, keep, ssm, scratch):
    with ExitStack() as ctx:
        sb = lambda n, s, t=F32: ctx.enter_context(nc.sbuf_tensor(n, s, t))
        sem = lambda n: ctx.enter_context(nc.semaphore(n))
        ps = [ctx.enter_context(nc.psum_tensor(f"in_ps{i}", [P, 512], F32)) for i in range(8)]
        w_in = sb("w_in", [P, DK, 2 * DI])
        w_x = sb("w_x", [P, DB, R + 2 * NS])
        w_dt = sb("w_dt", [R, DI])
        cw = sb("cw", [P, DB, TAPS])
        cb = sb("cb", [P, DB])
        dtb = sb("dtb", [P, DB])
        alog = sb("alog", [P, DB, NS])
        xT = sb("xT", [P, 2, DK, CH])
        HALO = TAPS - 1
        proj = sb("proj", [P, 2, DB, HALO + CH])
        conv = sb("conv", [P, DB, CH])
        u = keep["y"][:, 0:2 * DB, :].rearrange("p (a d) n -> p a d n", a=2)
        gate = keep["y"][:, 2 * DB:4 * DB, :].rearrange("p (a d) n -> p a d n", a=2)
        xdbc = sb("xdbc", [R + 2 * NS, CH])
        small = sb("small", [P, DB, CH])
        onep = sb("onep", [P, DB, CH])
        du = sb("du", [P, DB, CH])
        wl = sem("in_weights")
        xl = [sem("xT_even"), sem("xT_odd")]
        st = [sem("u_gate_stored_even"), sem("u_gate_stored_odd")]
        names = ("inproj_done", "inproj_out", "conv_step", "u_done", "halo_set", "xdbc_done", "xdbc_out", "bc_done",
                 "bc_out", "ring_done", "ring_out", "exp_z", "one_plus", "lost", "log_done", "delta_step", "du_done",
                 "a_exp", "a_set")
        s = {n: sem(n) for n in names}
        delta, duT, bc, A = ssm["delta"], ssm["duT"], ssm["bc"], ssm["A"]
        NU = 2 * DB

        def tok(c):
            return slice(c * CH, (c + 1) * CH)

        with nc.Block() as block:
            @block.sync
            def _(sp):
                def load_x(c):
                    if c >= 2:
                        sp.wait_ge(s["inproj_done"], NU * (c - 1))
                    sp.dma_start(xT[:, c % 2], io["xT"][:, tok(c)].rearrange("(k p) n -> p k n", p=P)).then_inc(
                        xl[c % 2], 16)
                sp.dma_start(w_in[:], io["WinT"].rearrange("(k p) n -> p k n", p=P)).then_inc(wl, 16)
                load_x(0)
                sp.dma_start(w_x[:], io["WxT"].rearrange("(k p) n -> p k n", p=P)).then_inc(wl, 16)
                sp.dma_start(w_dt[:], io["WdtT"]).then_inc(wl, 16)
                sp.dma_start(cw[:], io["conv_w"].rearrange("(k p) n -> p k n", p=P)).then_inc(wl, 16)
                with nc.allow_non_contiguous_dma(reason="512 values once"):
                    sp.dma_start(cb[:], io["conv_b"].rearrange("(k p) -> p k", p=P)).then_inc(wl, 16)
                    sp.dma_start(dtb[:], io["dt_bias"].rearrange("(k p) -> p k", p=P)).then_inc(wl, 16)
                sp.dma_start(alog[:], io["A_log"].rearrange("(k p) n -> p k n", p=P)).then_inc(wl, 16)
                load_x(1)
                for c in range(NC):
                    if c + 2 < NC:
                        load_x(c + 2)
                    sp.wait_ge(s["u_done"], c + 1)
                    sp.dma_start(scratch["ud"][c], u[:, c % 2]).then_inc(st[c % 2], 16)
                    sp.wait_ge(s["inproj_out"], NU * (c + 1))
                    sp.dma_start(scratch["gd"][c], gate[:, c % 2]).then_inc(st[c % 2], 16)
                for x in st:
                    sp.wait_ge(x, 32 * (NC // 2))

            @block.tensor
            def _(pe):
                ring = [0]

                def bank():
                    r = ring[0]
                    ring[0] += 1
                    if r >= 2:
                        pe.wait_ge(s["ring_out"], r - 1)
                    return ps[6 + r % 2]

                def inproj(c):
                    pe.wait_ge(xl[c % 2], 16 * (c // 2 + 1))
                    for m in range(NU):
                        j = NU * c + m
                        if j >= 4:
                            pe.wait_ge(s["inproj_out"], j - 3)
                        for k in range(DK):
                            mm = pe.matmul(ps[j % 4][:], w_in[:, k, m * P:(m + 1) * P], xT[:, c % 2, k, :],
                                           start=(k == 0), stop=(k == DK - 1))
                        mm.then_inc(s["inproj_done"], 1)

                def transpose_du(c):
                    pe.wait_ge(s["du_done"], c + 1)
                    for t in range(LT):
                        b = bank()
                        for d in range(DB):
                            mm = pe.transpose(b[:, d * P:(d + 1) * P], du[:, d, t * P:(t + 1) * P], keep["ident"][:])
                        mm.then_inc(s["ring_done"], 1)

                pe.wait_ge(wl, 16 * 7)
                inproj(0)
                for c in range(NC):
                    if c + 1 < NC:
                        inproj(c + 1)
                    if c:
                        transpose_du(c - 1)
                    pe.wait_ge(s["u_done"], c + 1)
                    if c:
                        pe.wait_ge(s["xdbc_out"], c)
                    for k in range(DB):
                        mm = pe.matmul(ps[4][0:R + 2 * NS, :], w_x[:, k, :], u[:, c % 2, k, :],
                                       start=(k == 0), stop=(k == DB - 1))
                    mm.then_inc(s["xdbc_done"], 1)
                    pe.wait_ge(s["xdbc_out"], c + 1)
                    if c:
                        pe.wait_ge(s["bc_out"], c)
                    n = R + 2 * NS
                    for t in range(LT):
                        mm = pe.transpose(ps[5][:, t * n:(t + 1) * n], xdbc[:, t * P:(t + 1) * P],
                                          keep["ident"][0:n, 0:n])
                    mm.then_inc(s["bc_done"], 1)
                    for m in range(DB):
                        b = bank()
                        pe.matmul(b[:], w_dt[:, m * P:(m + 1) * P], xdbc[0:R, :], start=True, stop=True).then_inc(
                            s["ring_done"], 1)
                transpose_du(NC - 1)

            @block.scalar
            def _(act):
                ring = [0]

                def bank():
                    r = ring[0]
                    ring[0] += 1
                    act.wait_ge(s["ring_done"], r + 1)
                    return ps[6 + r % 2]

                def proj_out(c):
                    for m in range(DB):
                        j = NU * c + m
                        act.wait_ge(s["inproj_done"], j + 1)
                        if c >= 2 and m == 0:
                            act.wait_ge(s["conv_step"], TAPS * DB * (c - 1))
                            act.wait_ge(s["halo_set"], c)
                        act.copy(proj[:, c % 2, m, HALO:], ps[j % 4][:]).then_inc(s["inproj_out"], 1)

                def gate_out(c):
                    for m in range(DB):
                        j = NU * c + DB + m
                        act.wait_ge(s["inproj_done"], j + 1)
                        if c >= 2 and m == 0:
                            act.wait_ge(st[c % 2], 32 * (c // 2))
                        act.activation(gate[:, c % 2, m, :], ps[j % 4][:], ACT.Silu).then_inc(s["inproj_out"], 1)

                def duT_out(c):
                    for t in range(LT):
                        b = bank()
                        act.copy(duT[:, LT * c + t, :], b[:]).then_inc(s["ring_out"], 1)

                act.wait_ge(wl, 16 * 7)
                act.activation(alog[:], alog[:], ACT.Exp).then_inc(s["a_exp"], 1)
                proj_out(0)
                gate_out(0)
                for c in range(NC):
                    if c + 1 < NC:
                        proj_out(c + 1)
                    act.wait_ge(s["conv_step"], TAPS * DB * (c + 1))
                    if c >= 2:
                        act.wait_ge(st[c % 2], 32 * (c // 2))
                        act.wait_ge(s["du_done"], c - 1)
                    act.activation(u[:, c % 2], conv[:], ACT.Silu).then_inc(s["u_done"], 1)
                    if c + 1 < NC:
                        gate_out(c + 1)
                    if c:
                        duT_out(c - 1)
                    act.wait_ge(s["xdbc_done"], c + 1)
                    if c:
                        act.wait_ge(s["bc_done"], c)
                        act.wait_ge(s["ring_done"], 8 * c - 4)
                    act.copy(xdbc[:], ps[4][0:R + 2 * NS, :]).then_inc(s["xdbc_out"], 1)
                    if c:
                        act.wait_ge(s["delta_step"], 2 * c)
                    for m in range(DB):
                        b = bank()
                        act.activation(small[:, m, :], b[:], ACT.Abs, bias=dtb[:, m:m + 1])
                        act.activation(delta[:, m, tok(c)], b[:], ACT.Relu, bias=dtb[:, m:m + 1]).then_inc(
                            s["ring_out"], 1)
                    act.wait_ge(s["ring_out"], ring[0])
                    act.activation(small[:], small[:], ACT.Exp, scale=-1.0).then_inc(s["exp_z"], 1)
                    act.wait_ge(s["lost"], c + 1)
                    act.activation(onep[:], onep[:], ACT.Ln).then_inc(s["log_done"], 1)
                duT_out(NC - 1)

            @block.gpsimd
            def _(pool):
                pool.memset(proj[:, 0, :, 0:HALO], 0.0).then_inc(s["halo_set"], 1)
                for c in range(NC - 1):
                    pool.wait_ge(s["inproj_out"], NU * c + DB)
                    if c >= 1:
                        pool.wait_ge(s["conv_step"], TAPS * DB * c)
                    pool.tensor_copy(proj[:, (c + 1) % 2, :, 0:HALO], proj[:, c % 2, :, CH:CH + HALO]).then_inc(
                        s["halo_set"], 1)

            @block.vector
            def _(dve):
                dve.wait_ge(wl, 16 * 7)
                dve.wait_ge(s["a_exp"], 1)
                dve.tensor_scalar(A[:], alog[:], -1.0, None, ALU.mult).then_inc(s["a_set"], 1)
                def convolve(c):
                    dve.wait_ge(s["halo_set"], c + 1)
                    if c:
                        dve.wait_ge(s["u_done"], c)
                    for k in reversed(range(TAPS)):
                        for m in range(DB):
                            step = TAPS * DB * c + DB * (TAPS - 1 - k) + m
                            src = proj[:, c % 2, m, k:k + CH]
                            if k == TAPS - 1:
                                dve.wait_ge(s["inproj_out"], NU * c + m + 1)
                                dve.tensor_scalar(conv[:, m, :], src, cw[:, m, k:k + 1], cb[:, m:m + 1],
                                                  ALU.mult, ALU.add).then_inc(s["conv_step"], 1)
                            else:
                                dve.wait_ge(s["conv_step"], step - DB + 1)
                                dve.scalar_tensor_tensor(conv[:, m, :], src, cw[:, m, k:k + 1], conv[:, m, :],
                                                         ALU.mult, ALU.add).then_inc(s["conv_step"], 1)

                convolve(0)
                for c in range(NC):
                    if c + 1 < NC:
                        convolve(c + 1)
                    dve.wait_ge(s["bc_done"], c + 1)
                    dve.tensor_copy(bc[:, LT * c:LT * (c + 1), :],
                                    ps[5][:, 0:LT * (R + 2 * NS)].rearrange("p (t n) -> p t n", t=LT)).then_inc(
                        s["bc_out"], 1)
                    dve.wait_ge(s["exp_z"], c + 1)
                    if c:
                        dve.wait_ge(s["delta_step"], 2 * c)
                    dve.tensor_scalar(onep[:], small[:], 1.0, None, ALU.add).then_inc(s["one_plus"], 1)
                    dve.wait_ge(s["one_plus"], c + 1)
                    dve.scalar_tensor_tensor(small[:], onep[:], -1.0, small[:], ALU.add, ALU.subtract).then_inc(
                        s["lost"], 1)
                    dve.wait_ge(s["log_done"], c + 1)
                    dve.tensor_tensor(onep[:], onep[:], small[:], ALU.subtract).then_inc(s["delta_step"], 1)
                    dve.wait_ge(s["delta_step"], 2 * c + 1)
                    dve.tensor_tensor(delta[:, :, tok(c)], delta[:, :, tok(c)], onep[:], ALU.add).then_inc(
                        s["delta_step"], 1)
                    dve.wait_ge(s["delta_step"], 2 * c + 2)
                    if c:
                        dve.wait_ge(s["ring_done"], 8 * c)
                    dve.tensor_tensor(du[:], delta[:, :, tok(c)], u[:, c % 2], ALU.mult).then_inc(s["du_done"], 1)


def ssm_scan(nc, io, keep, ssm, scratch):
    with ExitStack() as ctx:
        sb = lambda n, s, t=F32: ctx.enter_context(nc.sbuf_tensor(n, s, t))
        sem = lambda n: ctx.enter_context(nc.semaphore(n))
        bps = [ctx.enter_context(nc.psum_tensor(f"b_ps{i}", [P, CH], F32)) for i in range(DB)]
        hps = [ctx.enter_context(nc.psum_tensor(f"h_ps{i}", [P, DI], F32)) for i in range(LT)]
        dA = sb("dA", [P, 2, DB, CH])
        bT = sb("bT", [P, 2, LT, DI])
        h = sb("h", [P, 2, DB, CH])
        mi = sb("mi", [P, 2, S2], I32)
        mz = sb("mz", [P, 2, S2], BF16)
        macc = sb("macc", [P, S2])
        delta, duT, bc, A, y = ssm["delta"], ssm["duT"], ssm["bc"], ssm["A"], keep["y"]
        passed, bT_set, dA_set, b_in, scan_done, h_in, y_step, y_zero = (sem(n) for n in (
            "units_started", "bT_set", "dA_set", "b_in", "scan_done", "h_in", "y_step", "y_zero"))
        m_ld = [sem("mask_even"), sem("mask_odd")]
        m_st = [sem("masked_stored_even"), sem("masked_stored_odd")]
        m_is, m_add, m_cnt = sem("mask_zeros"), sem("mask_added"), sem("mask_counted")
        BN, CN = R, R + NS

        def looped(eng, body):
            body(0)
            with eng.Fori(1, NS) as n:
                body(n)

        def after(n, c, k):
            return n * (4 * NC) + (4 * c + k)

        with nc.Block() as block:
            def store(sp, t):
                sp.wait_ge(m_is, t + 1)
                sp.dma_start(scratch["md"][t * P:(t + 1) * P, :], mz[:, t % 2, :]).then_inc(m_st[t % 2], 16)

            @block.sync
            def _(sp):
                for t in range(L // P):
                    if t >= 2:
                        sp.wait_ge(m_is, t - 1)
                    sp.dma_start(mi[:, t % 2, :], io["mask"][t * P:(t + 1) * P, :]).then_inc(m_ld[t % 2], 16)
                    if t >= 1:
                        store(sp, t - 1)
                store(sp, L // P - 1)
                for x in m_st:
                    sp.wait_ge(x, 16 * (L // P // 2))

            @block.gpsimd
            def _(pool):
                pool.memset(macc[:], 0.0).then_inc(m_add, 1)
                for t in range(L // P):
                    pool.wait_ge(m_ld[t % 2], 16 * (t // 2 + 1))
                    if t >= 2:
                        pool.wait_ge(m_st[t % 2], 16 * (t // 2))
                        pool.wait_ge(m_add, t)
                    pool.tensor_scalar(mz[:, t % 2, :], mi[:, t % 2, :], 0.0, None, ALU.is_equal).then_inc(m_is, 1)
                    pool.wait_ge(m_is, t + 1)
                    pool.wait_ge(m_add, t + 1)
                    pool.tensor_tensor(macc[:], macc[:], mz[:, t % 2, :], ALU.add).then_inc(m_add, 1)

            @block.scalar
            def _(act):
                def body(n):
                    for c in range(NC):
                        for t in range(LT):
                            if t == 0 and not (isinstance(n, int) and c < 2):
                                act.wait_ge(b_in, after(n, c, -4))
                                wait_alone(act, scan_done, after(n, c, -4), passed)
                            act.mul(bT[:, c % 2, t, :], duT[:, LT * c + t, :],
                                    bc[:, LT * c + t, bass.ds(n + BN, 1)]).then_inc(bT_set, 1)
                        for d in range(DB):
                            act.activation(dA[:, c % 2, d, :], delta[:, d, c * CH:(c + 1) * CH], ACT.Exp,
                                           scale=A[:, d, bass.ds(n, 1)]).then_inc(dA_set, 1)
                looped(act, body)

            @block.tensor
            def _(pe):
                def transpose_b(n, c):
                    first = isinstance(n, int) and n == 0 and c == 0
                    pe.wait_ge(bT_set, after(n, c, 4))
                    for d in range(DB):
                        if not first:
                            pe.wait_ge(scan_done, after(n, c, d - 3))
                        for t in range(LT):
                            mm = pe.transpose(bps[d][:, t * P:(t + 1) * P], bT[:, c % 2, t, d * P:(d + 1) * P],
                                              keep["ident"][:])
                        mm.then_inc(b_in, 1)

                def transpose_h(n, c):
                    first = isinstance(n, int) and n == 0 and c == 0
                    pe.wait_ge(scan_done, after(n, c, 4))
                    for t in range(LT):
                        if not first:
                            pe.wait_ge(y_step, after(n, c, t - 3))
                        for d in range(DB):
                            mm = pe.transpose(hps[t][:, d * P:(d + 1) * P], h[:, c % 2, d, t * P:(t + 1) * P],
                                              keep["ident"][:])
                        mm.then_inc(h_in, 1)

                def body(n):
                    for c in range(NC):
                        transpose_b(n, c)
                        if c:
                            transpose_h(n, c - 1)
                        elif not (isinstance(n, int) and n == 0):
                            transpose_h(n - 1, NC - 1)
                looped(pe, body)
                transpose_h(NS - 1, NC - 1)

            @block.vector
            def _(dve):
                dve.memset(y[:], 0.0).then_inc(y_zero, 1)
                dve.wait_ge(y_zero, 1)

                def add_up(n, c, t):
                    dve.wait_ge(h_in, after(n, c, t + 1))
                    dve.scalar_tensor_tensor(y[:, LT * c + t, :], hps[t][:], bc[:, LT * c + t, bass.ds(n + CN, 1)],
                                             y[:, LT * c + t, :], ALU.mult, ALU.add).then_inc(y_step, 1)

                def scan(n, c, d):
                    dve.wait_ge(dA_set, after(n, c, d + 1))
                    dve.wait_ge(b_in, after(n, c, d + 1))
                    if d == 0 and not (isinstance(n, int) and c < 2):
                        dve.wait_ge(h_in, after(n, c, -4))
                    if not (isinstance(n, int) and c == 0):
                        dve.wait_ge(scan_done, after(n, c, d - 3))
                    start = 0.0 if c == 0 else h[:, (c - 1) % 2, d, CH - 1:CH]
                    dve.tensor_tensor_scan(h[:, c % 2, d, :], dA[:, c % 2, d, :], bps[d][:], start,
                                           ALU.mult, ALU.add).then_inc(scan_done, 1)

                def body(n):
                    for c in range(NC):
                        before = (n, c - 1) if c else (n - 1, NC - 1)
                        first = isinstance(n, int) and c == 0
                        scan(n, c, 0)
                        scan(n, c, 1)
                        if not first:
                            add_up(*before, 0)
                        scan(n, c, 2)
                        if not first:
                            add_up(*before, 1)
                        scan(n, c, 3)
                        if not first:
                            add_up(*before, 2)
                            add_up(*before, 3)
                looped(dve, body)
                for t in range(LT):
                    add_up(NS - 1, NC - 1, t)
                dve.wait_ge(m_add, L // P + 1)
                dve.tensor_reduce(keep["zeros"][:], macc[:], AX.X, ALU.add).then_inc(m_cnt, 1)


class Norm:

    def __init__(self, nc, ctx, name):
        sb = lambda n, s: ctx.enter_context(nc.sbuf_tensor(name + n, s, F32))
        self.stats = sb("_stats", [P, LT, 6])
        self.mv = sb("_mv", [P, LT, 2])
        self.std = sb("_std", [P, LT])
        self.step = ctx.enter_context(nc.semaphore(name + "_step"))
        self.root = ctx.enter_context(nc.semaphore(name + "_root"))
        self.steps = 2 * LT + 2

    def vector(self, dve, c, r, out, ready, inc):
        base = self.steps * c
        dve.wait_ge(*ready)
        for t in range(LT):
            dve.bn_stats(self.stats[:, t, :], r(t)).then_inc(self.step, 1)
        for t in range(LT):
            dve.wait_ge(self.step, base + t + 1)
            dve.bn_aggr(self.mv[:, t, :], self.stats[:, t, :]).then_inc(self.step, 1)
        dve.wait_ge(self.step, base + 2 * LT)
        dve.tensor_scalar(self.std[:], self.mv[:, :, 1], EPS, None, ALU.add).then_inc(self.step, 1)
        dve.wait_ge(self.root, c + 1)
        dve.reciprocal(self.std[:], self.std[:]).then_inc(self.step, 1)
        dve.wait_ge(self.step, base + 2 * LT + 2)
        for t in range(LT):
            dve.tensor_scalar(out(t), r(t), self.mv[:, t, 0:1], self.std[:, t:t + 1], ALU.subtract,
                              ALU.mult).then_inc(inc, 1)

    def scalar(self, act, c):
        act.wait_ge(self.step, self.steps * c + 2 * LT + 1)
        act.activation(self.std[:], self.std[:], ACT.Sqrt).then_inc(self.root, 1)


def ssm_output(nc, io, keep, scratch):
    with ExitStack() as ctx:
        sb = lambda n, s, t=F32: ctx.enter_context(nc.sbuf_tensor(n, s, t))
        sem = lambda n: ctx.enter_context(nc.semaphore(n))
        ps = [ctx.enter_context(nc.psum_tensor(f"out_ps{i}", [P, 512], F32)) for i in range(8)]
        w_out = sb("w_out", [P, DB, D])
        wq = sb("wq", [P, DK, D])
        dskip = sb("dskip", [P, DB])
        x = sb("x_res", [P, 2, LT, D])
        u = sb("u3", [P, 2, DB, CH])
        gate = sb("gate3", [P, 2, DB, CH])
        yg = sb("yg", [P, 2, DB, CH])
        r1 = sb("r1", [P, 2, LT, D])
        x1 = sb("x1", [P, 2, LT, D])
        x1T = sb("x1T", [P, DK, CH])
        qs = sb("qs", [P, DK, CH])
        qrest = sb("qrest", [P, DK, CH])
        qpart = sb("qpart", [P, DK, 3, CH], BF16)
        ones = sb("ones3", [P, 1])
        wl = sem("out_weights")
        ld = [sem("ug_even"), sem("ug_odd")]
        st = [sem("x1q_even"), sem("x1q_odd")]
        norm = Norm(nc, ctx, "n1")
        names = ("yT_done", "skip_done", "yg_done", "proj_done", "r_done", "x1_done", "x1T_in", "x1T_done", "q_in",
                 "q_out", "q1_done", "qrest_done", "q2_done", "q3_done", "flag_in", "flag_set", "ones_set")
        s = {n: sem(n) for n in names}
        y = keep["y"]
        Kg, k_ld = keep["Kg"], keep["keys_loaded"]

        with nc.Block() as block:
            @block.gpsimd
            def _(pool):
                pool.wait_ge(wl, 48)
                for v in ld:
                    pool.wait_ge(v, 48)
                for g in range(G):
                    heads = slice(g * HG, (g + 1) * HG)
                    for j, part in enumerate(KPART):
                        src = scratch["kd"][part, g * HG * HD:(g + 1) * HG * HD, :]
                        pool.dma_start(Kg[g][j * HD:(j + 1) * HD], src.rearrange("(h e) n -> e h n", h=HG)).then_inc(
                            k_ld[g], 16)
                    pool.dma_start(Kg[g][ONES0:ROWS_A], scratch["kbd"][:, heads, :]).then_inc(k_ld[g], 16)
                    pool.dma_start(Kg[g][ROWS_A:ROWS_B], io["ones"]).then_inc(k_ld[g], 16)

            @block.sync
            def _(sp):
                def load(c):
                    if c >= 2:
                        sp.wait_ge(s["yg_done"], c - 1)
                        sp.wait_ge(s["r_done"], 2 * (c - 1))
                    sp.dma_start(u[:, c % 2], scratch["ud"][c]).then_inc(ld[c % 2], 16)
                    sp.dma_start(gate[:, c % 2], scratch["gd"][c]).then_inc(ld[c % 2], 16)
                    sp.dma_start(x[:, c % 2], io["x"][c * CH:(c + 1) * CH, :].rearrange(
                        "(t p) n -> p t n", p=P)).then_inc(ld[c % 2], 16)
                sp.dma_start(w_out[:], io["WoutT"].rearrange("(k p) n -> p k n", p=P)).then_inc(wl, 16)
                with nc.allow_non_contiguous_dma(reason="512 values once"):
                    sp.dma_start(dskip[:], io["D_skip"].rearrange("(k p) -> p k", p=P)).then_inc(wl, 16)
                sp.dma_start(wq[:], io["WqT"].rearrange("(k p) n -> p k n", p=P)).then_inc(wl, 16)
                load(0)
                load(1)
                for c in range(NC):
                    if c + 2 < NC:
                        load(c + 2)
                    sp.wait_ge(s["x1_done"], LT * (c + 1))
                    sp.dma_start(scratch["x1d"][c * CH:(c + 1) * CH, :].rearrange("(t p) n -> p t n", p=P),
                                 x1[:, c % 2]).then_inc(st[c % 2], 16)
                    sp.wait_ge(s["q3_done"], DK * (c + 1))
                    for m in range(DK):
                        sp.dma_start(scratch["qd"][:, m * P:(m + 1) * P, c * CH:(c + 1) * CH].rearrange(
                            "j p n -> p j n"), qpart[:, m]).then_inc(st[c % 2], 16)
                for v in st:
                    sp.wait_ge(v, 48 * (NC // 2))
                sp.wait_ge(s["flag_set"], 1)

            @block.tensor
            def _(pe):
                def transpose_y(c):
                    for d in range(DB):
                        if c:
                            pe.wait_ge(s["skip_done"], DB * (c - 1) + d + 1)
                        for t in range(LT):
                            mm = pe.transpose(ps[d][:, t * P:(t + 1) * P], y[:, LT * c + t, d * P:(d + 1) * P],
                                              keep["ident"][:])
                        mm.then_inc(s["yT_done"], 1)

                pe.wait_ge(s["ones_set"], 1)
                pe.matmul(ps[7][0:1, 0:1], keep["zeros"][:], ones[:], start=True, stop=True).then_inc(s["flag_in"], 1)
                pe.wait_ge(wl, 48)
                def out_proj(c):
                    pe.wait_ge(s["yg_done"], c + 1)
                    for t in range(LT):
                        if c and t % 2 == 0:
                            pe.wait_ge(s["r_done"], 2 * (c - 1) + t // 2 + 1)
                        for k in range(DB):
                            mm = pe.matmul(ps[4 + t // 2][:, (t % 2) * D:(t % 2 + 1) * D],
                                           yg[:, c % 2, k, t * P:(t + 1) * P], w_out[:, k, :],
                                           start=(k == 0), stop=(k == DB - 1))
                        mm.then_inc(s["proj_done"], 1)

                def q_proj(c):
                    pe.wait_ge(s["x1_done"], LT * (c + 1))
                    if c:
                        pe.wait_ge(s["q_out"], DK * c)
                    else:
                        pe.wait_ge(s["flag_set"], 1)
                    for k in range(DK):
                        for t in range(LT):
                            mm = pe.transpose(ps[6 + k][:, t * P:(t + 1) * P], x1[:, c % 2, t, k * P:(k + 1) * P],
                                              keep["ident"][:])
                        mm.then_inc(s["x1T_in"], 1)
                    pe.wait_ge(s["x1T_done"], DK * (c + 1))
                    for m in range(DK):
                        for k in range(DK):
                            mm = pe.matmul(ps[6 + m][:], wq[:, k, m * P:(m + 1) * P], x1T[:, k, :],
                                           start=(k == 0), stop=(k == DK - 1))
                        mm.then_inc(s["q_in"], 1)

                transpose_y(0)
                out_proj(0)
                transpose_y(1)
                for c in range(NC):
                    if c + 1 < NC:
                        out_proj(c + 1)
                    if c + 2 < NC:
                        transpose_y(c + 2)
                    q_proj(c)

            @block.scalar
            def _(act):
                def first_part(c):
                    for k in range(DK):
                        act.wait_ge(s["x1T_in"], DK * c + k + 1)
                        if c:
                            act.wait_ge(s["q_in"], DK * c)
                        act.copy(x1T[:, k, :], ps[6 + k][:]).then_inc(s["x1T_done"], 1)
                    for m in range(DK):
                        act.wait_ge(s["q_in"], DK * c + m + 1)
                        if c:
                            act.wait_ge(s["qrest_done"], DK * (c - 1) + m + 1)
                        if c and m == 0:
                            act.wait_ge(st[(c - 1) % 2], 48 * ((c - 1) // 2 + 1))
                        act.mul(qs[:, m, :], ps[6 + m][:], float(HD) ** -0.5).then_inc(s["q_out"], 1)
                        act.wait_ge(s["q_out"], DK * c + m + 1)
                        act.copy(qpart[:, m, 0, :], qs[:, m, :]).then_inc(s["q1_done"], 1)

                def second_part(c):
                    for m in range(DK):
                        act.wait_ge(s["qrest_done"], DK * c + m + 1)
                        act.copy(qpart[:, m, 1, :], qrest[:, m, :]).then_inc(s["q2_done"], 1)

                for c in range(NC):
                    norm.scalar(act, c)
                    if c:
                        second_part(c - 1)
                    first_part(c)
                second_part(NC - 1)

            @block.vector
            def _(dve):
                dve.memset(ones[:], 1.0).then_inc(s["ones_set"], 1)
                dve.wait_ge(s["flag_in"], 1)
                dve.tensor_scalar(keep["flag"][:], ps[7][0:1, 0:1], 1.0, None, ALU.min).then_inc(s["flag_set"], 1)
                dve.wait_ge(wl, 48)

                def skip_gate(c):
                    dve.wait_ge(ld[c % 2], 48 * (c // 2 + 1))
                    if c >= 2:
                        dve.wait_ge(s["proj_done"], LT * (c - 1))
                    for d in range(DB):
                        dve.wait_ge(s["yT_done"], DB * c + d + 1)
                        dve.scalar_tensor_tensor(yg[:, c % 2, d, :], u[:, c % 2, d, :], dskip[:, d:d + 1], ps[d][:],
                                                 ALU.mult, ALU.add).then_inc(s["skip_done"], 1)
                    dve.wait_ge(s["skip_done"], DB * (c + 1))
                    dve.tensor_tensor(yg[:, c % 2], yg[:, c % 2], gate[:, c % 2], ALU.mult).then_inc(s["yg_done"], 1)

                def residual(c):
                    if c >= 2:
                        dve.wait_ge(s["x1_done"], LT * (c - 1))
                    for i in range(2):
                        dve.wait_ge(s["proj_done"], LT * c + 2 * (i + 1))
                        dve.tensor_tensor(r1[:, c % 2, 2 * i:2 * i + 2, :],
                                          ps[4 + i][:].rearrange("p (t n) -> p t n", t=2),
                                          x[:, c % 2, 2 * i:2 * i + 2, :], ALU.add).then_inc(s["r_done"], 1)

                def first_norm(c):
                    if c >= 2:
                        dve.wait_ge(st[c % 2], 48 * (c // 2))
                        dve.wait_ge(s["x1T_in"], DK * (c - 1))
                    norm.vector(dve, c, lambda t: r1[:, c % 2, t, :], lambda t: x1[:, c % 2, t, :],
                                (s["r_done"], 2 * (c + 1)), s["x1_done"])

                def split_q(c):
                    for m in range(DK):
                        dve.wait_ge(s["q1_done"], DK * c + m + 1)
                        if c:
                            dve.wait_ge(s["q3_done"], DK * (c - 1) + m + 1)
                        dve.tensor_tensor(qrest[:, m, :], qs[:, m, :], qpart[:, m, 0, :],
                                          ALU.subtract).then_inc(s["qrest_done"], 1)
                    for m in range(DK):
                        dve.wait_ge(s["q2_done"], DK * c + m + 1)
                        dve.tensor_tensor(qpart[:, m, 2, :], qrest[:, m, :], qpart[:, m, 1, :],
                                          ALU.subtract).then_inc(s["q3_done"], 1)

                skip_gate(0)
                residual(0)
                for c in range(NC):
                    if c + 1 < NC:
                        skip_gate(c + 1)
                    first_norm(c)
                    if c:
                        split_q(c - 1)
                    if c + 1 < NC:
                        residual(c + 1)
                split_q(NC - 1)


def attention(nc, io, keep, scratch, X):
    with ExitStack() as ctx:
        sb = lambda n, s, t=F32: ctx.enter_context(nc.sbuf_tensor(n, s, t))
        sem = lambda n: ctx.enter_context(nc.semaphore(n))
        pA = [ctx.enter_context(nc.psum_tensor(f"max_ps{i}", [P, 2, 512], F32)) for i in range(2)]
        pB = [ctx.enter_context(nc.psum_tensor(f"exp_ps{i}", [P, CH], F32)) for i in range(3)]
        pX = ctx.enter_context(nc.psum_tensor("pv_ps", [P, CH], F32))
        Kg, k_ld = keep["Kg"], keep["keys_loaded"]
        Qg = [sb(f"Qg{g}", [ROWS_B, HG, CH], BF16) for g in range(G)]
        PB = 4
        PT = sb("PT", [P, PB, HG, CH])
        NM = HG * LT
        half = sb("half", [P, 2, NM, 2])
        nmax = sb("nmax", [P, 2, NM])
        allm = sb("allm", [P, 2, NM])
        mrest = sb("mrest", [NM, 2, P])
        mpart = sb("mpart", [NM, 2, 3, P], BF16)
        MB = sb("MB", [P, 2 * LT, S2], BF16)
        negI = sb("negI", [P, P], BF16)
        V1 = keep["V1"]
        q_ld = [sem(f"Q{g}_loaded") for g in range(G)]
        m_ld = [sem(f"M{g}_loaded") for g in range(G)]
        names = ("mask_loaded", "q_ones", "a_done", "a_max", "half_step", "mT_done", "mT_read",
                 "m_step", "b_done", "exp_done", "pv_done", "x_out", "neg_loaded",
                 "x_started", "loads_started")
        s = {n: sem(n) for n in names}
        UA = 2 * NM
        UB = KT * HG
        NB = 3
        TB, TP, TX = 3, PB, 1

        def krows(t):
            return P if t < KT - 1 else KLAST

        with nc.Block() as block:
            def item(qc, g, per):
                return qc * (G * per) + g * per

            @block.sync
            def _(sp):
                def load_q(qc, g):
                    for j, part in enumerate(QPART):
                        src = scratch["qd"][part, g * HG * HD:(g + 1) * HG * HD, bass.ds(qc * CH, CH)]
                        sp.dma_start(Qg[g][j * HD:(j + 1) * HD], src.rearrange("(h e) n -> e h n", h=HG)).then_inc(
                            q_ld[g], 16)

                def load_mask(qc, at):
                    src = scratch["md"][bass.ds(qc * CH, CH), :].rearrange("(t p) n -> p t n", p=P)
                    sp.dma_start(MB[:, bass.ds(at, LT), :], src).then_inc(s["mask_loaded"], 16)

                def load_m(qc, g):
                    wait_alone(sp, s["m_step"], item(qc, g, 3) + 3, s["loads_started"])
                    for j in range(3):
                        sp.dma_start(Qg[g][ROWS_A + j:ROWS_A + j + 1], mpart[:, g % 2, j, :]).then_inc(m_ld[g], 16)

                load_q(0, 0)
                sp.dma_start(negI[:], io["negI"]).then_inc(s["neg_loaded"], 16)
                load_mask(0, 0)
                load_q(0, 1)
                load_m(0, 0)
                load_q(0, 2)
                load_q(0, 3)

                def chunk(qc, last):
                    if not last:
                        at = sp.snap((qc + 1) % 2 * LT)
                        wait_alone(sp, s["mask_loaded"], 16 * (qc + 1), s["loads_started"])
                    for g in range(G):
                        if not last and g == 0:
                            sp.wait_ge(s["b_done"], item(qc, g, UB) + 1)
                        if not (last and g == G - 1):
                            load_m(qc + (g + 1) // G, (g + 1) % G)
                        if not last:
                            if g == 0:
                                load_mask(qc + 1, at)
                            wait_alone(sp, s["b_done"], item(qc, g, UB) + UB, s["loads_started"])
                            load_q(qc + 1, g)

                with sp.Fori(0, NC - 1) as qc:
                    chunk(qc, False)
                chunk(NC - 1, True)

            @block.tensor
            def _(pe):
                def max_unit(qc, g, a, masked):
                    hh, t, hf = a // (2 * LT), a // 2 % LT, a % 2
                    if a == 0:
                        pe.wait_ge(q_ld[g], qc * (16 * NPAIR) + 16 * NPAIR)
                        if masked:
                            pe.wait_ge(s["mask_loaded"], qc * 16 + 16)
                    if not (isinstance(qc, int) and qc == 0 and g == 0 and a < 2):
                        pe.wait_ge(s["a_max"], item(qc, g, UA) + a - 1)
                    for j in range(2):
                        lo = MSTEP * (2 * hf + j)
                        out = pA[a % 2][:, j, 0:MW]
                        mm = pe.matmul(out, Qg[g][0:ROWS_A, hh, t * P:(t + 1) * P], Kg[g][0:ROWS_A, hh, lo:lo + MW],
                                       start=True, stop=not masked)
                        if masked:
                            mm = pe.matmul(out, negI[:], MB[:, bass.ds((qc % 2) * LT + t, 1), lo:lo + MW],
                                           start=False, stop=True)
                    mm.then_inc(s["a_done"], 1)

                def max_rows(qc, g):
                    pe.wait_ge(s["half_step"], item(qc, g, 3) + 3)
                    pe.transpose(pA[0][0:NM, 0, 0:P], nmax[:, g % 2, :], keep["ident"][:]).then_inc(s["mT_done"], 1)

                def exp_unit(qc, g, t, hh, masked):
                    b = t * HG + hh
                    if b == 0:
                        pe.wait_ge(m_ld[g], qc * 48 + 48)
                    back = NB if b >= NB else {0: 1, 1: 3, 2: 2}[b]
                    pe.wait_ge(s["exp_done"], item(qc, g, UB) + (b - back + 1 if b >= NB else 1 - back) + TB)
                    out = pB[b % NB][0:krows(t)]
                    mm = pe.matmul(out, Kg[g][:, hh, t * P:t * P + krows(t)], Qg[g][:, hh, :],
                                   start=True, stop=not masked)
                    if masked:
                        for qt in range(LT):
                            mm = pe.matmul(out[:, qt * P:(qt + 1) * P],
                                           MB[:, bass.ds((qc % 2) * LT + qt, 1), t * P:t * P + krows(t)], negI[:],
                                           start=False, stop=(qt == LT - 1))
                    mm.then_inc(s["b_done"], 1)

                def values(qc, g, t):
                    pe.wait_ge(s["exp_done"], item(qc, g, UB) + HG * (t + 1) + TB)
                    if t == 0:
                        pe.wait_ge(s["x_out"], item(qc, g, 1) + TX)
                    for hh in range(HG):
                        mm = pe.matmul(pX[2 * HD * hh:2 * HD * (hh + 1), :],
                                       V1[0:krows(t), t, g * HG + hh, :],
                                       PT[0:krows(t), (KT * g + t) % PB, hh, :],
                                       start=(t == 0), stop=(t == KT - 1), skip_group_check=True)
                    mm.then_inc(s["pv_done"], 1)

                def chunk(qc, last, masked):
                    nc.disable_value_cache = masked
                    for g in range(G):
                        run(qc, g, last, masked)
                    nc.disable_value_cache = False

                def run(qc, g, last, masked):
                    qa, ga = qc + (g + 2) // G, (g + 2) % G
                    ahead = not (last and g >= G - 2)
                    a = 0
                    for t in range(KT):
                        hh = 0
                        for step in "EMEMVEME":
                            if step == "E":
                                exp_unit(qc, g, t, hh, masked)
                                hh += 1
                            elif step == "M" and ahead and a < (t + 1) * UA // KT:
                                if a == 4:
                                    pe.wait_ge(s["mT_read"], item(qc, g, 1) + 2)
                                max_unit(qa, ga, a, masked)
                                a += 1
                            elif step == "V" and t >= 2:
                                values(qc, g, t - 2)
                            elif step == "V" and g > 0:
                                values(qc, g - 1, KT - 2 + t)
                        if t == 1 and not (last and g == G - 1):
                            if ahead:
                                pe.wait_ge(s["a_max"], item(qa, ga, UA) + 3)
                            max_rows(qc + (g + 1) // G, (g + 1) % G)
                    if ahead:
                        assert a == UA
                    if g == G - 1:
                        for t in (KT - 2, KT - 1):
                            values(qc, g, t)

                def start(masked):
                    for a in range(UA):
                        max_unit(0, 0, a, masked)
                    max_rows(0, 0)
                    pe.wait_ge(s["mT_read"], 1)
                    for a in range(UA):
                        max_unit(0, 1, a, masked)

                pe.wait_ge(s["neg_loaded"], 16)
                pe.wait_ge(s["q_ones"], 16 * G)
                for g in range(G):
                    pe.wait_ge(k_ld[g], 16 * (NPAIR + 2))
                zeros = pe.value_load(keep["flag"][0:1, 0:1], min_val=0, max_val=1)
                with pe.If(zeros > 0):
                    start(True)
                with pe.Else():
                    start(False)
                with pe.Fori(0, NC - 1) as qc:
                    with pe.If(zeros > 0):
                        chunk(qc, False, True)
                    with pe.Else():
                        chunk(qc, False, False)
                with pe.If(zeros > 0):
                    chunk(NC - 1, True, True)
                with pe.Else():
                    chunk(NC - 1, True, False)

            @block.scalar
            def _(act):
                for g in range(G):
                    act.dma_start(Qg[g][ONES0:ROWS_A], io["ones"][:, 0:HG, 0:CH]).then_inc(s["q_ones"], 16)
                act.sem_inc(s["exp_done"], TB)

                def x_from_psum(qc, g):
                    wait_alone(act, s["pv_done"], item(qc, g, KT) + KT + TP, s["x_started"])
                    act.copy(X[:, g, bass.ds(qc * CH, CH)], pX[:]).then_inc(s["x_out"], 1)

                def run(qc, g):
                    for t in range(KT):
                        for hh in range(HG):
                            b = t * HG + hh
                            act.wait_ge(s["b_done"], item(qc, g, UB) + b + 1)
                            if hh == 0:
                                act.wait_ge(s["pv_done"], item(qc, g, KT) + t - PB + 1 + TP)
                            act.activation(PT[0:krows(t), (KT * g + t) % PB, hh, :], pB[b % NB][0:krows(t)],
                                           ACT.Exp).then_inc(s["exp_done"], 1)
                        if t == 1 and g > 0:
                            x_from_psum(qc, g - 1)
                    if g == G - 1:
                        x_from_psum(qc, g)

                with act.Fori(0, NC) as qc:
                    for g in range(G):
                        run(qc, g)

            @block.vector
            def _(dve):
                dve.sem_inc(s["x_out"], TX)
                dve.sem_inc(s["pv_done"], TP)

                def maxima(qc, g, lo, hi):
                    for a in range(lo, hi):
                        dve.wait_ge(s["a_done"], item(qc, g, UA) + a + 1)
                        if a == 0 and not (isinstance(qc, int) and qc == 0 and g < 2):
                            dve.wait_ge(s["half_step"], item(qc, g, 3) - 3)
                        dve.tensor_reduce(half[:, g % 2, a // 2, a % 2:a % 2 + 1], pA[a % 2][:, :, 0:MW], AX.XY,
                                          ALU.max, negate=True).then_inc(s["a_max"], 1)

                def both(qc, g):
                    dve.wait_ge(s["a_max"], item(qc, g, UA) + UA)
                    if not (isinstance(qc, int) and qc == 0 and g < 2):
                        dve.wait_ge(s["mT_done"], item(qc, g, 1) - 1)
                    dve.tensor_reduce(nmax[:, g % 2, :], half[:, g % 2], AX.X, ALU.min).then_inc(s["half_step"], 1)
                    dve.wait_ge(s["half_step"], item(qc, g, 3) + 1)
                    dve.tensor_scalar(allm[:, g % 2, :], nmax[:, g % 2, :], MASKED / 2, 3e38, ALU.is_gt,
                                      ALU.mult).then_inc(s["half_step"], 1)
                    dve.wait_ge(s["half_step"], item(qc, g, 3) + 2)
                    dve.scalar_tensor_tensor(nmax[:, g % 2, :], allm[:, g % 2, :], 3e38, nmax[:, g % 2, :],
                                             ALU.mult, ALU.add).then_inc(s["half_step"], 1)

                def split(qc, g):
                    pm = pA[0][0:NM, 0, 0:P]
                    part = mpart[:, g % 2]
                    rest = mrest[:, g % 2, :]
                    at = item(qc, g, 3)
                    dve.wait_ge(s["mT_done"], item(qc, g, 1) + 1)
                    if isinstance(qc, int) and qc == 0 and g < 2:
                        pass
                    elif g >= 2:
                        dve.wait_ge(m_ld[g - 2], qc * 48 + 48)
                    else:
                        dve.wait_ge(m_ld[g + 2], qc * 48)
                    dve.tensor_copy(part[:, 0, :], pm).then_inc(s["m_step"], 1)
                    dve.wait_ge(s["m_step"], at + 1)
                    dve.tensor_tensor(rest, pm, part[:, 0, :], ALU.subtract).then_inc(s["mT_read"], 1)
                    dve.wait_ge(s["mT_read"], item(qc, g, 1) + 1)
                    dve.tensor_copy(part[:, 1, :], rest).then_inc(s["m_step"], 1)
                    dve.wait_ge(s["m_step"], at + 2)
                    dve.tensor_tensor(part[:, 2, :], rest, part[:, 1, :], ALU.subtract).then_inc(s["m_step"], 1)

                def run(qc, g, last):
                    qa, ga = qc + (g + 2) // G, (g + 2) % G
                    ahead = not (last and g >= G - 2)
                    if ahead:
                        maxima(qa, ga, 0, 4)
                    if not (last and g == G - 1):
                        split(qc + (g + 1) // G, (g + 1) % G)
                    if ahead:
                        maxima(qa, ga, 4, UA)
                        both(qa, ga)

                maxima(0, 0, 0, UA)
                both(0, 0)
                split(0, 0)
                maxima(0, 1, 0, UA)
                both(0, 1)
                with dve.Fori(0, NC - 1) as qc:
                    for g in range(G):
                        run(qc, g, False)
                for g in range(G):
                    run(NC - 1, g, True)


def tail(nc, io, keep, scratch, X, out):
    with ExitStack() as ctx:
        sb = lambda n, s, t=F32: ctx.enter_context(nc.sbuf_tensor(n, s, t))
        sem = lambda n: ctx.enter_context(nc.semaphore(n))
        ps = [ctx.enter_context(nc.psum_tensor(f"t_ps{i}", [P, 512], F32)) for i in range(8)]
        sel = sb("sel", [P, P])
        wo = sb("wo", [P, G, D])
        gates = ("f", "i", "c")
        w = {g: sb(f"ffn_w{g}", [P, DK, D]) for g in (*gates, "o")}
        uw = {g: sb(f"ffn_u{g}", [P, DK, D]) for g in (*gates, "o")}
        gb = sb("gb", [P, 3, DK])
        bo = sb("bo", [1, D])
        onerow = sb("onerow", [1, P])
        c0 = sb("c0", [P, DK])
        x1 = sb("x1r", [P, 2, LT, D])
        den = sb("den", [P, L * H // P])
        on = sb("on", [P, G, CH])
        r2 = sb("r2", [P, LT, D])
        x2 = sb("x2", [P, 2, LT, D])
        x2T = sb("x2T", [P, DK, CH])
        act_g = {g: sb(f"act_{g}", [P, DK, CH]) for g in gates}
        ig = sb("ig", [P, DK, CH])
        cs = sb("cs", [P, DK, CH])
        hh = sb("hh", [P, LT, D])
        res = sb("res", [P, 2, LT, D])
        wl = sem("gate_weights")
        wl_o = sem("out_proj_weights")
        den_ld = sem("sums_gathered")
        rec_ld = sem("reciprocals_in_place")
        ld = [sem("x1_even"), sem("x1_odd")]
        st = [sem("out_even"), sem("out_odd")]
        norm2, norm3 = Norm(nc, ctx, "n2"), Norm(nc, ctx, "n3")
        names = ("row_set", "gb_in", "gb_set", "sum_done", "den_done", "on_done", "proj_done", "r_done", "x2_done",
                 "x2T_in", "x2T_done", "gate_in", "gate_done", "ig_done", "c_done", "h_in", "h_done", "r3_done",
                 "res_done")
        s = {n: sem("t_" + n) for n in names}
        NW = 1 + 2 * 4 + 3 + 1
        NG = 3 * DK

        with nc.Block() as block:
            @block.sync
            def _(sp):
                def load(c):
                    if c >= 2:
                        sp.wait_ge(s["r_done"], 2 * (c - 1))
                    sp.dma_start(x1[:, c % 2], scratch["x1d"][c * CH:(c + 1) * CH, :].rearrange(
                        "(t p) n -> p t n", p=P)).then_inc(ld[c % 2], 16)

                for h in range(HG):
                    row = 2 * HD * h + HD
                    sp.dma_start(den[P // HG * h:P // HG * (h + 1), :], X[row:row + 1, :, :].rearrange(
                        "o g (b n) -> o (g b) n", n=L * H // P)).then_inc(den_ld, 16)
                sp.dma_start(sel[:], io["sel"]).then_inc(wl_o, 16)
                sp.dma_start(wo[:], io["WoP"].rearrange("g p n -> p g n")).then_inc(wl_o, 16)
                sp.wait_ge(s["den_done"], 2)
                for h in range(HG):
                    row = 2 * HD * h + HD
                    sp.dma_start(X[row:row + 1, :, :].rearrange("o g (b n) -> o (g b) n", n=L * H // P),
                                 den[P // HG * h:P // HG * (h + 1), :]).then_inc(rec_ld, 16)
                load(0)
                sp.dma_start(bo[:], io["bo"]).then_inc(wl, 16)
                for g in (*gates, "o"):
                    sp.dma_start(w[g][:], io[f"w{g}T"].rearrange("(k p) n -> p k n", p=P)).then_inc(wl, 16)
                    sp.dma_start(uw[g][:], io[f"u{g}T"].rearrange("(k p) n -> p k n", p=P)).then_inc(wl, 16)
                with nc.allow_non_contiguous_dma(reason="256 values once"):
                    for j, g in enumerate(gates):
                        sp.dma_start(gb[:, j, :], io[f"b{g}"].rearrange("(k p) -> p k", p=P)).then_inc(wl, 16)
                    sp.dma_start(c0[:], io["in_c"].rearrange("(k p) -> p k", p=P)).then_inc(wl, 16)

                load(1)
                for c in range(NC):
                    if c >= 1 and c + 1 < NC:
                        load(c + 1)
                    sp.wait_ge(s["res_done"], LT * (c + 1))
                    sp.dma_start(out[c * CH:(c + 1) * CH, :].rearrange("(t p) n -> p t n", p=P),
                                 res[:, c % 2]).then_inc(st[c % 2], 16)
                for v in st:
                    sp.wait_ge(v, 16 * (NC // 2))

            @block.gpsimd
            def _(pool):
                pool.memset(onerow[:], 1.0).then_inc(s["row_set"], 1)

            @block.tensor
            def _(pe):
                def state_bias():
                    pe.wait_ge(wl, 16 * NW)
                    for j, g in enumerate(gates):
                        for m in range(DK):
                            for k in range(DK):
                                mm = pe.matmul(ps[6][:, j * DK + m:j * DK + m + 1], uw[g][:, k, m * P:(m + 1) * P],
                                               c0[:, k:k + 1], start=(k == 0), stop=(k == DK - 1))
                    mm.then_inc(s["gb_in"], 1)

                def sums(c):
                    for g in range(G):
                        j = G * c + g
                        if j >= 2:
                            pe.wait_ge(s["on_done"], j - 1)
                        pe.matmul(ps[j % 2][:], sel[:], X[:, g, c * CH:(c + 1) * CH], start=True,
                                  stop=True).then_inc(s["sum_done"], 1)

                def out_proj(c):
                    pe.wait_ge(s["on_done"], G * (c + 1))
                    for t in range(LT):
                        if c and t % 2 == 0:
                            pe.wait_ge(s["r_done"], 2 * (c - 1) + t // 2 + 1)
                        for g in range(G):
                            mm = pe.matmul(ps[2 + t // 2][:, (t % 2) * D:(t % 2 + 1) * D],
                                           on[:, g, t * P:(t + 1) * P], wo[:, g, :], start=(g == 0),
                                           stop=(g == G - 1))
                        mm.then_inc(s["proj_done"], 1)

                def gate_products(c):
                    pe.wait_ge(s["x2_done"], LT * (c + 1))
                    if c:
                        pe.wait_ge(s["h_done"], 2 * c)
                    for k in range(DK):
                        for t in range(LT):
                            mm = pe.transpose(ps[4 + k][:, t * P:(t + 1) * P], x2[:, c % 2, t, k * P:(k + 1) * P],
                                              keep["ident"][:])
                        mm.then_inc(s["x2T_in"], 1)
                    pe.wait_ge(s["x2T_done"], DK * (c + 1))
                    for j, g in enumerate(gates):
                        for m in range(DK):
                            r = NG * c + DK * j + m
                            if r >= 2:
                                pe.wait_ge(s["gate_done"], r - 1)
                            elif r == 0:
                                pe.wait_ge(s["gb_set"], 1)
                            for k in range(DK):
                                mm = pe.matmul(ps[6 + r % 2][:], w[g][:, k, m * P:(m + 1) * P], x2T[:, k, :],
                                               start=(k == 0), stop=(k == DK - 1))
                            mm.then_inc(s["gate_in"], 1)

                def h_products(c):
                    for t in range(LT):
                        o = ps[4 + t // 2][:, (t % 2) * D:(t % 2 + 1) * D]
                        for k in range(DK):
                            pe.matmul(o, x2T[:, k, t * P:(t + 1) * P], w["o"][:, k, :], start=(k == 0), stop=False)
                        if t == 0:
                            pe.wait_ge(s["c_done"], c + 1)
                        for k in range(DK):
                            pe.matmul(o, cs[:, k, t * P:(t + 1) * P], uw["o"][:, k, :], start=False, stop=False)
                        pe.matmul(o, onerow[:], bo[:], start=False, stop=True).then_inc(s["h_in"], 1)

                pe.wait_ge(s["row_set"], 1)
                pe.wait_ge(wl_o, 32)
                pe.wait_ge(rec_ld, 16 * HG)
                sums(0)
                out_proj(0)
                sums(1)
                state_bias()
                for c in range(NC):
                    gate_products(c)
                    if c + 1 < NC:
                        out_proj(c + 1)
                    h_products(c)
                    if c + 2 < NC:
                        sums(c + 2)

            @block.scalar
            def _(act):
                norm2.scalar(act, 0)
                for c in range(NC):
                    for k in range(DK):
                        act.wait_ge(s["x2T_in"], DK * c + k + 1)
                        if c:
                            act.wait_ge(s["h_in"], LT * c)
                        act.copy(x2T[:, k, :], ps[4 + k][:]).then_inc(s["x2T_done"], 1)
                    if c:
                        norm3.scalar(act, c - 1)
                        act.wait_ge(s["c_done"], c)
                    else:
                        act.wait_ge(s["gb_set"], 1)
                    for j, g in enumerate(gates):
                        for m in range(DK):
                            r = NG * c + DK * j + m
                            act.wait_ge(s["gate_in"], r + 1)
                            act.activation(act_g[g][:, m, :], ps[6 + r % 2][:], ACT.Tanh if g == "c" else ACT.Sigmoid,
                                           bias=gb[:, j, m:m + 1]).then_inc(s["gate_done"], 1)
                    if c + 1 < NC:
                        norm2.scalar(act, c + 1)
                    for i in range(2):
                        act.wait_ge(s["h_in"], LT * c + 2 * (i + 1))
                        if c:
                            act.wait_ge(s["res_done"], LT * c)
                        act.activation(hh[:, 2 * i:2 * i + 2, :], ps[4 + i][:].rearrange("p (t n) -> p t n", t=2),
                                       ACT.Tanh).then_inc(s["h_done"], 1)
                norm3.scalar(act, NC - 1)

            @block.vector
            def _(dve):
                dve.wait_ge(den_ld, 16 * HG)
                dve.tensor_scalar(den[:], den[:], 1.0, None, ALU.add).then_inc(s["den_done"], 1)
                dve.wait_ge(s["den_done"], 1)
                dve.reciprocal(den[:], den[:]).then_inc(s["den_done"], 1)

                def divide(c):
                    dve.wait_ge(rec_ld, 16 * HG)
                    if c:
                        dve.wait_ge(s["proj_done"], LT * c)
                    for g in range(G):
                        j = G * c + g
                        dve.wait_ge(s["sum_done"], j + 1)
                        dve.tensor_tensor(on[:, g, :], X[:, g, c * CH:(c + 1) * CH], ps[j % 2][:],
                                          ALU.mult).then_inc(s["on_done"], 1)

                def second_norm(c):
                    dve.wait_ge(ld[c % 2], 16 * (c // 2 + 1))
                    if c:
                        dve.wait_ge(s["x2_done"], LT * c)
                    for i in range(2):
                        dve.wait_ge(s["proj_done"], LT * c + 2 * (i + 1))
                        dve.tensor_tensor(r2[:, 2 * i:2 * i + 2, :],
                                          ps[2 + i][:].rearrange("p (t n) -> p t n", t=2),
                                          x1[:, c % 2, 2 * i:2 * i + 2, :], ALU.add).then_inc(s["r_done"], 1)
                    if c >= 2:
                        dve.wait_ge(s["r3_done"], c - 1)
                    norm2.vector(dve, c, lambda t: r2[:, t, :], lambda t: x2[:, c % 2, t, :],
                                 (s["r_done"], 2 * (c + 1)), s["x2_done"])

                def cell(c):
                    dve.wait_ge(s["gate_done"], NG * (c + 1))
                    if c:
                        dve.wait_ge(s["h_in"], LT * c)
                    dve.tensor_tensor(ig[:], act_g["i"][:], act_g["c"][:], ALU.mult).then_inc(s["ig_done"], 1)
                    dve.wait_ge(s["ig_done"], c + 1)
                    for m in range(DK):
                        last = dve.scalar_tensor_tensor(cs[:, m, :], act_g["f"][:, m, :], c0[:, m:m + 1], ig[:, m, :],
                                                        ALU.mult, ALU.add)
                    last.then_inc(s["c_done"], 1)

                def third_norm(c):
                    dve.wait_ge(s["h_done"], 2 * (c + 1))
                    dve.tensor_tensor(hh[:], hh[:], x2[:, c % 2], ALU.add).then_inc(s["r3_done"], 1)
                    if c >= 2:
                        dve.wait_ge(st[c % 2], 16 * (c // 2))
                    norm3.vector(dve, c, lambda t: hh[:, t, :], lambda t: res[:, c % 2, t, :],
                                 (s["r3_done"], c + 1), s["res_done"])

                divide(0)
                second_norm(0)
                divide(1)
                dve.wait_ge(wl, 16 * NW)
                dve.wait_ge(s["gb_in"], 1)
                dve.tensor_tensor(gb[:], gb[:], ps[6][:, 0:NG].rearrange("p (j m) -> p j m", j=3),
                                  ALU.add).then_inc(s["gb_set"], 1)
                for c in range(NC):
                    cell(c)
                    if c + 1 < NC:
                        second_norm(c + 1)
                    if c + 2 < NC:
                        divide(c + 2)
                    third_norm(c)


def program(nc, io, out):
    scratch = {}
    for name, shape, t in (("kd", [3, D, S2], BF16), ("kbd", [3, H, S2], BF16), ("qd", [3, D, L], BF16),
                           ("md", [L, S2], BF16), ("ud", [NC, P, DB, CH], F32), ("gd", [NC, P, DB, CH], F32),
                           ("x1d", [L, D], F32)):
        scratch[name] = nc.dram_tensor("scratch_" + name, shape, t, kind="Internal").ap()
    with ExitStack() as ctx:
        keep = {
            "ident": ctx.enter_context(nc.sbuf_tensor("ident", [P, P], F32)),
            "V1": ctx.enter_context(nc.sbuf_tensor("V1", [P, KT, H, 2 * HD], F32)),
            "zeros": ctx.enter_context(nc.sbuf_tensor("zeros", [P, 1], F32)),
            "flag": ctx.enter_context(nc.sbuf_tensor("flag", [1, 1], I32)),
        }
        keys_values(nc, io, keep, scratch)
        y = ctx.enter_context(nc.sbuf_tensor("y_or_X", [P, L // P, DI], F32))
        X = y[:].rearrange("p t n -> p (t n)").rearrange("p (g n) -> p g n", g=G)
        keep["y"] = y
        with ExitStack() as ssm_ctx:
            ssm = {n: ssm_ctx.enter_context(nc.sbuf_tensor(n, shape, F32)) for n, shape in (
                ("delta", [P, DB, L]), ("duT", [P, L // P, DI]), ("bc", [P, L // P, R + 2 * NS]),
                ("A", [P, DB, NS]))}
            ssm_inputs(nc, io, keep, ssm, scratch)
            ssm_scan(nc, io, keep, ssm, scratch)
        with ExitStack() as key_ctx:
            keep["Kg"] = [key_ctx.enter_context(nc.sbuf_tensor(f"Kg{g}", [ROWS_B, HG, S2], BF16)) for g in range(G)]
            keep["keys_loaded"] = [key_ctx.enter_context(nc.semaphore(f"K{g}_loaded")) for g in range(G)]
            ssm_output(nc, io, keep, scratch)
            attention(nc, io, keep, scratch, X)
        tail(nc, io, keep, scratch, X, out)


def kernel(**inputs):
    import numpy as np
    import ml_dtypes
    import concourse.bacc as bacc
    from concourse.bass_utils import run_bass_kernel_spmd as launch

    g = {k: np.asarray(v) for k, v in inputs.items()}
    wo_rows = np.zeros((G, P, D), np.float32)
    woT = g["L0_xattn_W_o"].T
    for h in range(H):
        wo_rows[h // HG, 2 * HD * (h % HG):2 * HD * (h % HG) + HD] = woT[h * HD:(h + 1) * HD]
    sel = np.zeros((P, P), np.float32)
    for h in range(HG):
        sel[2 * HD * h + HD, 2 * HD * h:2 * HD * h + HD] = 1.0
    ratio = 2.0 ** (-8.0 / H)
    arrays = {
        "x": g["x"][0], "xT": g["x"][0].T, "ctxT": g["ctx_1024"][0].T, "kpos": g["itok_BxS2_1_8191"],
        "mask": g["mask_BxSxS2_if1"][0],
        "WinT": g["L0_attn_W_in"].T, "conv_w": g["L0_attn_conv_w"], "conv_b": g["L0_attn_conv_b"],
        "WxT": g["L0_attn_W_x"].T, "WdtT": g["L0_attn_W_dt"].T, "dt_bias": g["L0_attn_dt_bias"],
        "A_log": g["L0_attn_A_log"], "D_skip": g["L0_attn_D_skip"], "WoutT": g["L0_attn_W_out"].T,
        "WqT": g["L0_xattn_W_q"].T, "WkT": g["L0_xattn_W_k"].T, "WvT": g["L0_xattn_W_v"].T, "WoP": wo_rows,
        "bo": g["L0_ffn_bo"][None], "in_c": g["L0_ffn_in_c"],
        "ident": np.eye(P, dtype=np.float32), "sel": sel,
        "negI": (-MASKED * np.eye(P, dtype=np.float32)).astype(ml_dtypes.bfloat16),
        "ones": np.ones((3, HG, S2), ml_dtypes.bfloat16),
        "slopes": np.array([[ratio ** i] for i in range(1, H + 1)], np.float32),
    }
    for n in "fico":
        arrays[f"w{n}T"] = g[f"L0_ffn_w{n}"].T
        arrays[f"u{n}T"] = g[f"L0_ffn_u{n}"].T
        if n != "o":
            arrays[f"b{n}"] = g[f"L0_ffn_b{n}"]
    arrays = {k: np.ascontiguousarray(v) for k, v in arrays.items()}
    nc = bacc.Bacc("TRN2", target_bir_lowering=False, num_devices=1)
    io = {k: nc.dram_tensor("in_" + k, v.shape, mybir.dt.from_np(v.dtype), kind="ExternalInput").ap()
          for k, v in arrays.items()}
    out = nc.dram_tensor("out", [L, D], F32, kind="ExternalOutput").ap()
    program(nc, io, out)
    r = launch(nc, [{"in_" + k: v for k, v in arrays.items()}], core_ids=[0])
    return r.results[0]["out"].reshape(1, L, D)
```

```python
import concourse.bass as bass
from concourse import mybir
from contextlib import ExitStack

F32 = mybir.dt.float32
BF16 = mybir.dt.bfloat16
I32 = mybir.dt.int32
ALU = mybir.AluOpType
ACT = mybir.ActivationFunctionType
AX = mybir.AxisListType

P = 128
L = 2048
D = 256
DI = 512
NS = 16
R = 16
TAPS = 4
S2 = 1601
H = 16
HD = D // H
CH = 512
NC = L // CH
LT = CH // P
DB = DI // P
DK = D // P
KT = (S2 + P - 1) // P
KLAST = S2 - (KT - 1) * P
HG = 4
G = H // HG
EPS = 1e-5
QPART = (0, 0, 1, 1, 0, 2)
KPART = (0, 1, 0, 1, 2, 0)
NPAIR = len(QPART)
ROWS_A = NPAIR * HD + 3
ROWS_B = ROWS_A + 3
ONES0 = NPAIR * HD
MW = 401
MSTEP = 400
MASKED = 2.0 ** 100


def wait_alone(eng, sem, value, passed):
    eng.wait_ge(sem, value)
    eng.sem_inc(passed, 1)


def keys_values(nc, io, keep, inputs, delta, scratch):
    with ExitStack() as ctx:
        sb = lambda n, s, t=F32: ctx.enter_context(nc.sbuf_tensor(n, s, t))
        sem = lambda n: ctx.enter_context(nc.semaphore(n))
        ps = [ctx.enter_context(nc.psum_tensor(f"kv_ps{i}", [P, 512], F32)) for i in range(8)]
        flat = delta[:].rearrange("p d n -> p (d n)")
        ctxT, krest = (flat[:, i * DK * S2:(i + 1) * DK * S2].rearrange("p (k n) -> p k n", k=DK) for i in range(2))
        wk = sb("wk", [P, DK, D])
        wv = sb("wv", [P, DK, D])
        kpart = sb("kpart", [P, DK, 3, S2], BF16)
        pos = sb("pos", [H, S2], I32)
        kb = sb("kb", [H, S2])
        kbrest = sb("kbrest", [H, S2])
        kbpart = sb("kbpart", [H, 3, S2], BF16)
        slopes = sb("slopes", [H, 1])
        pmax = sb("pmax", [H, 1])
        loaded, pos_loaded = sem("kv_loaded"), sem("pos_loaded")
        ctx_loaded = [sem(f"context{n}_loaded") for n in range(4)]
        k_done, v_done, k1_done, r_done, k2_done, k3_done = (sem(n) for n in (
            "k_done", "v_done", "k1_done", "krest_done", "k2_done", "k3_done"))
        v_out, v1_set, bias_step, stored = sem("v_out"), sem("v1_set"), sem("bias_step"), sem("kv_stored")
        V1 = keep["V1"]
        cuts = [(n * 512, min(512, S2 - n * 512)) for n in range(4)]
        units = [(m, n) for n in range(4) for m in range(DK)]

        with nc.Block() as block:
            @block.sync
            def _(sp):
                sp.dma_start(wk[:], io["WkT"].rearrange("(k p) n -> p k n", p=P)).then_inc(loaded, 16)
                sp.dma_start(pos[:], io["kpos"].broadcast_to([H, S2])).then_inc(pos_loaded, 16)
                sp.dma_start(slopes[:], io["slopes"]).then_inc(pos_loaded, 16)
                for n, (lo, w) in enumerate(cuts):
                    sp.dma_start(ctxT[:, :, lo:lo + w], io["ctxT"][:, lo:lo + w].rearrange(
                        "(k p) n -> p k n", p=P)).then_inc(ctx_loaded[n], 16)
                sp.dma_start(wv[:], io["WvT"].rearrange("(k p) n -> p k n", p=P)).then_inc(loaded, 16)
                sp.dma_start(keep["ident"][:], io["ident"]).then_inc(pos_loaded, 16)
                load_inputs(nc, sp, io, inputs)
                sp.wait_ge(k3_done, len(units))
                for m in range(DK):
                    sp.dma_start(scratch["kd"][:, m * P:(m + 1) * P, :].rearrange("j p n -> p j n"),
                                 kpart[:, m, :, :]).then_inc(stored, 16)
                sp.wait_ge(bias_step, 7)
                sp.dma_start(scratch["kbd"].rearrange("j h n -> h j n"), kbpart[:]).then_inc(stored, 16)
                sp.wait_ge(stored, 48)
                sp.wait_ge(pos_loaded, 48)

            @block.gpsimd
            def _(pool):
                pool.memset(V1[:, :, :, HD:], 0.0).then_inc(v1_set, 1)
                pool.wait_ge(v1_set, 1)
                pool.memset(V1[:, :, :, HD:HD + 1], 1.0).then_inc(v1_set, 1)

            @block.tensor
            def _(pe):
                pe.wait_ge(loaded, 32)
                for u, (m, n) in enumerate(units):
                    lo, w = cuts[n]
                    pe.wait_ge(ctx_loaded[n], 16)
                    for k in range(DK):
                        mm = pe.matmul(ps[u][:, 0:w], wk[:, k, m * P:(m + 1) * P], ctxT[:, k, lo:lo + w],
                                       start=(k == 0), stop=(k == DK - 1))
                    mm.then_inc(k_done, 1)
                for t in range(KT):
                    rows = P if t < KT - 1 else KLAST
                    if t < 8:
                        pe.wait_ge(r_done, t + 1)
                    else:
                        pe.wait_ge(v_out, t - 7)
                    for k in range(DK):
                        mm = pe.matmul(ps[t % 8][0:rows, 0:D], ctxT[:, k, t * P:t * P + rows], wv[:, k, :],
                                       start=(k == 0), stop=(k == DK - 1))
                    mm.then_inc(v_done, 1)

            def second(act, u):
                m, n = units[u]
                lo, w = cuts[n]
                act.wait_ge(r_done, u + 1)
                act.copy(kpart[:, m, 1, lo:lo + w], krest[:, m, lo:lo + w]).then_inc(k2_done, 1)

            @block.scalar
            def _(act):
                for u, (m, n) in enumerate(units):
                    lo, w = cuts[n]
                    act.wait_ge(k_done, u + 1)
                    act.copy(kpart[:, m, 0, lo:lo + w], ps[u][:, 0:w]).then_inc(k1_done, 1)
                    if u:
                        second(act, u - 1)
                second(act, len(units) - 1)
                for t in range(KT):
                    rows = P if t < KT - 1 else KLAST
                    act.wait_ge(v_done, t + 1)
                    act.copy(V1[0:rows, t, :, 0:HD],
                             ps[t % 8][0:rows, 0:D].rearrange("p (h e) -> p h e", h=H)).then_inc(v_out, 1)

            @block.vector
            def _(dve):
                dve.wait_ge(pos_loaded, 48)
                dve.tensor_copy(kb[:], pos[:]).then_inc(bias_step, 1)
                dve.wait_ge(bias_step, 1)
                dve.tensor_reduce(pmax[:], kb[:], AX.X, ALU.max).then_inc(bias_step, 1)
                dve.wait_ge(bias_step, 2)
                dve.tensor_scalar(kb[:], kb[:], pmax[:], slopes[:], ALU.subtract, ALU.mult).then_inc(bias_step, 1)
                dve.wait_ge(bias_step, 3)
                dve.tensor_copy(kbpart[:, 0, :], kb[:]).then_inc(bias_step, 1)
                dve.wait_ge(bias_step, 4)
                dve.tensor_tensor(kbrest[:], kb[:], kbpart[:, 0, :], ALU.subtract).then_inc(bias_step, 1)
                dve.wait_ge(bias_step, 5)
                dve.tensor_copy(kbpart[:, 1, :], kbrest[:]).then_inc(bias_step, 1)
                dve.wait_ge(bias_step, 6)
                dve.tensor_tensor(kbpart[:, 2, :], kbrest[:], kbpart[:, 1, :], ALU.subtract).then_inc(bias_step, 1)
                for u, (m, n) in enumerate(units):
                    lo, w = cuts[n]
                    dve.wait_ge(k1_done, u + 1)
                    dve.tensor_tensor(krest[:, m, lo:lo + w], ps[u][:, 0:w], kpart[:, m, 0, lo:lo + w],
                                      ALU.subtract).then_inc(r_done, 1)
                for u, (m, n) in enumerate(units):
                    lo, w = cuts[n]
                    dve.wait_ge(k2_done, u + 1)
                    dve.tensor_tensor(kpart[:, m, 2, lo:lo + w], krest[:, m, lo:lo + w],
                                      kpart[:, m, 1, lo:lo + w], ALU.subtract).then_inc(k3_done, 1)


def input_buffers(nc, ctx, duT):
    sb = lambda n, s: ctx.enter_context(nc.sbuf_tensor(n, s, F32))
    buffers = {n: sb(n, shape) for n, shape in (
        ("w_x", [P, DB, R + 2 * NS]), ("w_dt", [R, DI]), ("cw", [P, DB, TAPS]),
        ("cb", [P, DB]), ("dtb", [P, DB]), ("alog", [P, DB, NS]))}
    chunk = lambda c: duT[:, LT * c:LT * (c + 1), :].rearrange("p t n -> p (t n)")
    buffers["w_in"] = chunk(NC - 1).rearrange("p (k n) -> p k n", k=DK)
    buffers["xT"] = chunk(NC - 2).rearrange("p (a k n) -> p a k n", a=2, k=DK)
    buffers["loaded"] = ctx.enter_context(nc.semaphore("in_weights"))
    buffers["x_loaded"] = [ctx.enter_context(nc.semaphore(n)) for n in ("xT_even", "xT_odd")]
    return buffers


def load_inputs(nc, sp, io, b):
    wl = b["loaded"]

    def load_x(c):
        sp.dma_start(b["xT"][:, c], io["xT"][:, c * CH:(c + 1) * CH].rearrange("(k p) n -> p k n", p=P)).then_inc(
            b["x_loaded"][c], 16)
    sp.dma_start(b["w_in"], io["WinT"].rearrange("(k p) n -> p k n", p=P)).then_inc(wl, 16)
    load_x(0)
    sp.dma_start(b["w_x"][:], io["WxT"].rearrange("(k p) n -> p k n", p=P)).then_inc(wl, 16)
    sp.dma_start(b["w_dt"][:], io["WdtT"]).then_inc(wl, 16)
    sp.dma_start(b["cw"][:], io["conv_w"].rearrange("(k p) n -> p k n", p=P)).then_inc(wl, 16)
    with nc.allow_non_contiguous_dma(reason="512 values once"):
        sp.dma_start(b["cb"][:], io["conv_b"].rearrange("(k p) -> p k", p=P)).then_inc(wl, 16)
        sp.dma_start(b["dtb"][:], io["dt_bias"].rearrange("(k p) -> p k", p=P)).then_inc(wl, 16)
    sp.dma_start(b["alog"][:], io["A_log"].rearrange("(k p) n -> p k n", p=P)).then_inc(wl, 16)
    load_x(1)


def ssm_inputs(nc, io, keep, inputs, ssm, scratch):
    with ExitStack() as ctx:
        sb = lambda n, s, t=F32: ctx.enter_context(nc.sbuf_tensor(n, s, t))
        sem = lambda n: ctx.enter_context(nc.semaphore(n))
        ps = [ctx.enter_context(nc.psum_tensor(f"in_ps{i}", [P, 512], F32)) for i in range(8)]
        w_in, w_x, w_dt, cw, cb, dtb, alog, xT = (inputs[n] for n in (
            "w_in", "w_x", "w_dt", "cw", "cb", "dtb", "alog", "xT"))
        HALO = TAPS - 1
        proj = sb("proj", [P, 2, DB, HALO + CH])
        conv = sb("conv", [P, DB, CH])
        u = keep["y"][:, 0:2 * DB, :].rearrange("p (a d) n -> p a d n", a=2)
        gate = keep["y"][:, 2 * DB:4 * DB, :].rearrange("p (a d) n -> p a d n", a=2)
        xdbc = sb("xdbc", [R + 2 * NS, CH])
        small = sb("small", [P, DB, CH])
        onep = sb("onep", [P, DB, CH])
        du = sb("du", [P, DB, CH])
        wl, xl = inputs["loaded"], inputs["x_loaded"]
        st = [sem("u_gate_stored_even"), sem("u_gate_stored_odd")]
        names = ("inproj_done", "inproj_out", "conv_step", "u_done", "halo_set", "xdbc_done", "xdbc_out", "bc_done",
                 "bc_out", "ring_done", "ring_out", "exp_z", "one_plus", "lost", "log_done", "delta_step", "du_done",
                 "a_exp", "a_set")
        s = {n: sem(n) for n in names}
        delta, duT, bc, A = ssm["delta"], ssm["duT"], ssm["bc"], ssm["A"]
        NU = 2 * DB
        halves = (slice(0, DB // 2), slice(DB // 2, DB))

        def tok(c):
            return slice(c * CH, (c + 1) * CH)

        with nc.Block() as block:
            @block.sync
            def _(sp):
                def load_x(c):
                    sp.wait_ge(s["inproj_done"], NU * (c - 1))
                    sp.dma_start(xT[:, c % 2], io["xT"][:, tok(c)].rearrange("(k p) n -> p k n", p=P)).then_inc(
                        xl[c % 2], 16)
                for c in range(NC):
                    if c + 2 < NC:
                        load_x(c + 2)
                    sp.wait_ge(s["u_done"], c + 1)
                    sp.dma_start(scratch["ud"][c], u[:, c % 2]).then_inc(st[c % 2], 16)
                    sp.wait_ge(s["inproj_out"], NU * (c + 1))
                    sp.dma_start(scratch["gd"][c], gate[:, c % 2]).then_inc(st[c % 2], 16)
                for x in st:
                    sp.wait_ge(x, 32 * (NC // 2))

            @block.tensor
            def _(pe):
                ring = [0]

                def bank():
                    r = ring[0]
                    ring[0] += 1
                    if r >= 2:
                        pe.wait_ge(s["ring_out"], r - 1)
                    return ps[6 + r % 2]

                def inproj(c, half):
                    pe.wait_ge(xl[c % 2], 16 * (c // 2 + 1))
                    for m in range(half * DB, (half + 1) * DB):
                        j = NU * c + m
                        if j >= 4:
                            pe.wait_ge(s["inproj_out"], j - 3)
                        for k in range(DK):
                            mm = pe.matmul(ps[j % 4][:], w_in[:, k, m * P:(m + 1) * P], xT[:, c % 2, k, :],
                                           start=(k == 0), stop=(k == DK - 1))
                        mm.then_inc(s["inproj_done"], 1)

                def transpose_du(c):
                    pe.wait_ge(s["du_done"], 2 * (c + 1))
                    for t in range(LT):
                        b = bank()
                        for d in range(DB):
                            mm = pe.transpose(b[:, d * P:(d + 1) * P], du[:, d, t * P:(t + 1) * P], keep["ident"][:])
                        mm.then_inc(s["ring_done"], 1)

                pe.wait_ge(wl, 16 * 7)
                inproj(0, 0)
                inproj(0, 1)
                for c in range(NC):
                    if c + 1 < NC:
                        inproj(c + 1, 0)
                    pe.wait_ge(s["u_done"], c + 1)
                    if c:
                        pe.wait_ge(s["xdbc_out"], c)
                    for k in range(DB):
                        mm = pe.matmul(ps[4][0:R + 2 * NS, :], w_x[:, k, :], u[:, c % 2, k, :],
                                       start=(k == 0), stop=(k == DB - 1))
                    mm.then_inc(s["xdbc_done"], 1)
                    pe.wait_ge(s["xdbc_out"], c + 1)
                    if c:
                        pe.wait_ge(s["bc_out"], c)
                    n = R + 2 * NS
                    for t in range(LT):
                        mm = pe.transpose(ps[5][:, t * n:(t + 1) * n], xdbc[:, t * P:(t + 1) * P],
                                          keep["ident"][0:n, 0:n])
                    mm.then_inc(s["bc_done"], 1)
                    for m in range(DB):
                        b = bank()
                        pe.matmul(b[:], w_dt[:, m * P:(m + 1) * P], xdbc[0:R, :], start=True, stop=True).then_inc(
                            s["ring_done"], 1)
                    if c:
                        transpose_du(c - 1)
                    if c + 1 < NC:
                        inproj(c + 1, 1)
                transpose_du(NC - 1)

            @block.scalar
            def _(act):
                ring = [0]

                def bank():
                    r = ring[0]
                    ring[0] += 1
                    act.wait_ge(s["ring_done"], r + 1)
                    return ps[6 + r % 2]

                def proj_out(c):
                    for m in range(DB):
                        j = NU * c + m
                        act.wait_ge(s["inproj_done"], j + 1)
                        if c >= 2 and m == 0:
                            act.wait_ge(s["conv_step"], TAPS * DB * (c - 1))
                            act.wait_ge(s["halo_set"], c)
                        act.copy(proj[:, c % 2, m, HALO:], ps[j % 4][:]).then_inc(s["inproj_out"], 1)

                def gate_out(c):
                    for m in range(DB):
                        j = NU * c + DB + m
                        act.wait_ge(s["inproj_done"], j + 1)
                        if c >= 2 and m == 0:
                            act.wait_ge(st[c % 2], 32 * (c // 2))
                        act.activation(gate[:, c % 2, m, :], ps[j % 4][:], ACT.Silu).then_inc(s["inproj_out"], 1)

                def duT_out(c):
                    for t in range(LT):
                        b = bank()
                        act.copy(duT[:, LT * c + t, :], b[:]).then_inc(s["ring_out"], 1)

                act.wait_ge(wl, 16 * 7)
                act.activation(alog[:], alog[:], ACT.Exp).then_inc(s["a_exp"], 1)
                proj_out(0)
                gate_out(0)
                for c in range(NC):
                    act.wait_ge(s["conv_step"], TAPS * DB * (c + 1))
                    if c >= 2:
                        act.wait_ge(st[c % 2], 32 * (c // 2))
                        act.wait_ge(s["du_done"], 2 * (c - 1))
                    act.activation(u[:, c % 2], conv[:], ACT.Silu).then_inc(s["u_done"], 1)
                    if c + 1 < NC:
                        proj_out(c + 1)
                    act.wait_ge(s["xdbc_done"], c + 1)
                    if c:
                        act.wait_ge(s["bc_done"], c)
                        act.wait_ge(s["ring_done"], max(DB, (DB + LT) * (c - 1)))
                    act.copy(xdbc[:], ps[4][0:R + 2 * NS, :]).then_inc(s["xdbc_out"], 1)
                    if c:
                        act.wait_ge(s["delta_step"], 4 * c)
                    for i, half in enumerate(halves):
                        for m in range(half.start, half.stop):
                            b = bank()
                            act.activation(small[:, m, :], b[:], ACT.Abs, bias=dtb[:, m:m + 1])
                            act.activation(delta[:, m, tok(c)], b[:], ACT.Relu, bias=dtb[:, m:m + 1]).then_inc(
                                s["ring_out"], 1)
                        act.wait_ge(s["ring_out"], ring[0])
                        act.activation(small[:, half], small[:, half], ACT.Exp, scale=-1.0).then_inc(s["exp_z"], 1)
                    if c:
                        duT_out(c - 1)
                    for i, half in enumerate(halves):
                        act.wait_ge(s["lost"], 2 * c + i + 1)
                        act.activation(onep[:, half], onep[:, half], ACT.Ln).then_inc(s["log_done"], 1)
                    if c + 1 < NC:
                        gate_out(c + 1)
                duT_out(NC - 1)

            @block.gpsimd
            def _(pool):
                pool.memset(proj[:, 0, :, 0:HALO], 0.0).then_inc(s["halo_set"], 1)
                for c in range(NC - 1):
                    pool.wait_ge(s["inproj_out"], NU * c + DB)
                    if c >= 1:
                        pool.wait_ge(s["conv_step"], TAPS * DB * c)
                    pool.tensor_copy(proj[:, (c + 1) % 2, :, 0:HALO], proj[:, c % 2, :, CH:CH + HALO]).then_inc(
                        s["halo_set"], 1)

            @block.vector
            def _(dve):
                dve.wait_ge(wl, 16 * 7)
                dve.wait_ge(s["a_exp"], 1)
                dve.tensor_scalar(A[:], alog[:], -1.0, None, ALU.mult).then_inc(s["a_set"], 1)
                def convolve(c):
                    dve.wait_ge(s["halo_set"], c + 1)
                    if c:
                        dve.wait_ge(s["u_done"], c)
                    for k in reversed(range(TAPS)):
                        for m in range(DB):
                            step = TAPS * DB * c + DB * (TAPS - 1 - k) + m
                            src = proj[:, c % 2, m, k:k + CH]
                            if k == TAPS - 1:
                                dve.wait_ge(s["inproj_out"], NU * c + m + 1)
                                dve.tensor_scalar(conv[:, m, :], src, cw[:, m, k:k + 1], cb[:, m:m + 1],
                                                  ALU.mult, ALU.add).then_inc(s["conv_step"], 1)
                            else:
                                dve.wait_ge(s["conv_step"], step - DB + 1)
                                dve.scalar_tensor_tensor(conv[:, m, :], src, cw[:, m, k:k + 1], conv[:, m, :],
                                                         ALU.mult, ALU.add).then_inc(s["conv_step"], 1)

                convolve(0)
                for c in range(NC):
                    if c + 1 < NC:
                        convolve(c + 1)
                    dve.wait_ge(s["bc_done"], c + 1)
                    dve.tensor_copy(bc[:, LT * c:LT * (c + 1), :],
                                    ps[5][:, 0:LT * (R + 2 * NS)].rearrange("p (t n) -> p t n", t=LT)).then_inc(
                        s["bc_out"], 1)
                    for i, half in enumerate(halves):
                        dve.wait_ge(s["exp_z"], 2 * c + i + 1)
                        if c:
                            dve.wait_ge(s["delta_step"], 4 * c)
                        dve.tensor_scalar(onep[:, half], small[:, half], 1.0, None, ALU.add).then_inc(
                            s["one_plus"], 1)
                        dve.wait_ge(s["one_plus"], 2 * c + i + 1)
                        dve.scalar_tensor_tensor(small[:, half], onep[:, half], -1.0, small[:, half], ALU.add,
                                                 ALU.subtract).then_inc(s["lost"], 1)
                    for i, half in enumerate(halves):
                        dve.wait_ge(s["log_done"], 2 * c + i + 1)
                        dve.tensor_tensor(onep[:, half], onep[:, half], small[:, half], ALU.subtract).then_inc(
                            s["delta_step"], 1)
                        dve.wait_ge(s["delta_step"], 4 * c + 2 * i + 1)
                        dve.tensor_tensor(delta[:, half, tok(c)], delta[:, half, tok(c)], onep[:, half],
                                          ALU.add).then_inc(s["delta_step"], 1)
                        dve.wait_ge(s["delta_step"], 4 * c + 2 * i + 2)
                        if c:
                            dve.wait_ge(s["ring_done"], (DB + LT) * c + DB)
                        dve.tensor_tensor(du[:, half], delta[:, half, tok(c)], u[:, c % 2, half], ALU.mult).then_inc(
                            s["du_done"], 1)


def ssm_scan(nc, io, keep, ssm, early, scratch):
    with ExitStack() as ctx:
        sb = lambda n, s, t=F32: ctx.enter_context(nc.sbuf_tensor(n, s, t))
        sem = lambda n: ctx.enter_context(nc.semaphore(n))
        bps = [ctx.enter_context(nc.psum_tensor(f"b_ps{i}", [P, CH], F32)) for i in range(DB)]
        hps = [ctx.enter_context(nc.psum_tensor(f"h_ps{i}", [P, DI], F32)) for i in range(LT)]
        dA = sb("dA", [P, 2, DB, CH])
        bT = sb("bT", [P, 2, LT, DI])
        h = sb("h", [P, 2, DB, CH])
        MH = (S2 + 1) // 2
        MT = 2 * (L // P)
        mi = sb("mi", [P, 2, MH], I32)
        mz = sb("mz", [P, 2, MH], BF16)
        macc = sb("macc", [P, MH], BF16)
        delta, duT, bc, A, y = ssm["delta"], ssm["duT"], ssm["bc"], ssm["A"], keep["y"]
        passed, bT_set, dA_set, b_in, scan_done, h_in, y_step, y_zero = (sem(n) for n in (
            "units_started", "bT_set", "dA_set", "b_in", "scan_done", "h_in", "y_step", "y_zero"))
        m_ld = [sem("mask_even"), sem("mask_odd")]
        m_st = [sem("masked_stored_even"), sem("masked_stored_odd")]
        m_is, m_add, m_cnt = sem("mask_zeros"), sem("mask_added"), sem("mask_counted")
        BN, CN = R, R + NS

        def looped(eng, body):
            body(0)
            with eng.Fori(1, NS) as n:
                body(n)

        def after(n, c, k):
            return n * (4 * NC) + (4 * c + k)

        with nc.Block() as block:
            def part(t, array):
                lo, hi = t % 2 * MH, min(S2, (t % 2 + 1) * MH)
                return array[t // 2 * P:(t // 2 + 1) * P, lo:hi], hi - lo

            def store(sp, t):
                sp.wait_ge(m_is, t + 1)
                tile, width = part(t, scratch["md"])
                sp.dma_start(tile, mz[:, t % 2, 0:width]).then_inc(m_st[t % 2], 16)

            @block.sync
            def _(sp):
                for t in range(MT):
                    if t >= 2:
                        sp.wait_ge(m_is, t - 1)
                    tile, width = part(t, io["mask"])
                    sp.dma_start(mi[:, t % 2, 0:width], tile).then_inc(m_ld[t % 2], 16)
                    if t >= 1:
                        store(sp, t - 1)
                    if t == 2:
                        load_early(nc, sp, io, scratch, early)
                store(sp, MT - 1)
                for x in m_st:
                    sp.wait_ge(x, 16 * (MT // 2))

            @block.gpsimd
            def _(pool):
                pool.memset(macc[:], 0.0).then_inc(m_add, 1)
                for t in range(MT):
                    width = part(t, io["mask"])[1]
                    pool.wait_ge(m_ld[t % 2], 16 * (t // 2 + 1))
                    if t >= 2:
                        pool.wait_ge(m_st[t % 2], 16 * (t // 2))
                        pool.wait_ge(m_add, t)
                    pool.tensor_scalar(mz[:, t % 2, 0:width], mi[:, t % 2, 0:width], 0.0, None,
                                       ALU.is_equal).then_inc(m_is, 1)
                    pool.wait_ge(m_is, t + 1)
                    pool.wait_ge(m_add, t + 1)
                    pool.tensor_tensor(macc[:, 0:width], macc[:, 0:width], mz[:, t % 2, 0:width],
                                       ALU.add).then_inc(m_add, 1)

            @block.scalar
            def _(act):
                def body(n):
                    for c in range(NC):
                        for t in range(LT):
                            if t == 0 and not (isinstance(n, int) and c < 2):
                                act.wait_ge(b_in, after(n, c, -4))
                                wait_alone(act, scan_done, after(n, c, -4), passed)
                            act.mul(bT[:, c % 2, t, :], duT[:, LT * c + t, :],
                                    bc[:, LT * c + t, bass.ds(n + BN, 1)]).then_inc(bT_set, 1)
                        for d in range(DB):
                            act.activation(dA[:, c % 2, d, :], delta[:, d, c * CH:(c + 1) * CH], ACT.Exp,
                                           scale=A[:, d, bass.ds(n, 1)]).then_inc(dA_set, 1)
                looped(act, body)

            @block.tensor
            def _(pe):
                def transpose_b(n, c):
                    first = isinstance(n, int) and n == 0 and c == 0
                    pe.wait_ge(bT_set, after(n, c, 4))
                    for d in range(DB):
                        if not first:
                            pe.wait_ge(scan_done, after(n, c, d - 3))
                        for t in range(LT):
                            mm = pe.transpose(bps[d][:, t * P:(t + 1) * P], bT[:, c % 2, t, d * P:(d + 1) * P],
                                              keep["ident"][:])
                        mm.then_inc(b_in, 1)

                def transpose_h(n, c):
                    first = isinstance(n, int) and n == 0 and c == 0
                    pe.wait_ge(scan_done, after(n, c, 4))
                    for t in range(LT):
                        if not first:
                            pe.wait_ge(y_step, after(n, c, t - 3))
                        for d in range(DB):
                            mm = pe.transpose(hps[t][:, d * P:(d + 1) * P], h[:, c % 2, d, t * P:(t + 1) * P],
                                              keep["ident"][:])
                        mm.then_inc(h_in, 1)

                def body(n):
                    for c in range(NC):
                        transpose_b(n, c)
                        if c:
                            transpose_h(n, c - 1)
                        elif not (isinstance(n, int) and n == 0):
                            transpose_h(n - 1, NC - 1)
                looped(pe, body)
                transpose_h(NS - 1, NC - 1)

            @block.vector
            def _(dve):
                dve.memset(y[:], 0.0).then_inc(y_zero, 1)
                dve.wait_ge(y_zero, 1)

                def add_up(n, c, t):
                    dve.wait_ge(h_in, after(n, c, t + 1))
                    dve.scalar_tensor_tensor(y[:, LT * c + t, :], hps[t][:], bc[:, LT * c + t, bass.ds(n + CN, 1)],
                                             y[:, LT * c + t, :], ALU.mult, ALU.add).then_inc(y_step, 1)

                def scan(n, c, d):
                    dve.wait_ge(dA_set, after(n, c, d + 1))
                    dve.wait_ge(b_in, after(n, c, d + 1))
                    if d == 0 and not (isinstance(n, int) and c < 2):
                        dve.wait_ge(h_in, after(n, c, -4))
                    if not (isinstance(n, int) and c == 0):
                        dve.wait_ge(scan_done, after(n, c, d - 3))
                    start = 0.0 if c == 0 else h[:, (c - 1) % 2, d, CH - 1:CH]
                    dve.tensor_tensor_scan(h[:, c % 2, d, :], dA[:, c % 2, d, :], bps[d][:], start,
                                           ALU.mult, ALU.add).then_inc(scan_done, 1)

                def body(n):
                    for c in range(NC):
                        before = (n, c - 1) if c else (n - 1, NC - 1)
                        first = isinstance(n, int) and c == 0
                        scan(n, c, 0)
                        scan(n, c, 1)
                        if not first:
                            add_up(*before, 0)
                        scan(n, c, 2)
                        if not first:
                            add_up(*before, 1)
                        scan(n, c, 3)
                        if not first:
                            add_up(*before, 2)
                            add_up(*before, 3)
                looped(dve, body)
                for t in range(LT):
                    add_up(NS - 1, NC - 1, t)
                dve.wait_ge(m_add, MT + 1)
                dve.tensor_reduce(keep["zeros"][:], macc[:], AX.X, ALU.add).then_inc(m_cnt, 1)


class Norm:

    def __init__(self, nc, ctx, name):
        sb = lambda n, s: ctx.enter_context(nc.sbuf_tensor(name + n, s, F32))
        self.stats = sb("_stats", [P, LT, 6])
        self.mv = sb("_mv", [P, LT, 2])
        self.std = sb("_std", [P, LT])
        self.step = ctx.enter_context(nc.semaphore(name + "_step"))
        self.root = ctx.enter_context(nc.semaphore(name + "_root"))
        self.steps = 2 * LT + 2

    def vector(self, dve, c, r, out, ready, inc):
        base = self.steps * c
        dve.wait_ge(*ready)
        for t in range(LT):
            dve.bn_stats(self.stats[:, t, :], r(t)).then_inc(self.step, 1)
        for t in range(LT):
            dve.wait_ge(self.step, base + t + 1)
            dve.bn_aggr(self.mv[:, t, :], self.stats[:, t, :]).then_inc(self.step, 1)
        dve.wait_ge(self.step, base + 2 * LT)
        dve.tensor_scalar(self.std[:], self.mv[:, :, 1], EPS, None, ALU.add).then_inc(self.step, 1)
        dve.wait_ge(self.root, c + 1)
        dve.reciprocal(self.std[:], self.std[:]).then_inc(self.step, 1)
        dve.wait_ge(self.step, base + 2 * LT + 2)
        for t in range(LT):
            dve.tensor_scalar(out(t), r(t), self.mv[:, t, 0:1], self.std[:, t:t + 1], ALU.subtract,
                              ALU.mult).then_inc(inc, 1)

    def scalar(self, act, c):
        act.wait_ge(self.step, self.steps * c + 2 * LT + 1)
        act.activation(self.std[:], self.std[:], ACT.Sqrt).then_inc(self.root, 1)


def early_buffers(nc, ctx):
    b = {n: ctx.enter_context(nc.sbuf_tensor(n, shape, F32)) for n, shape in (
        ("w_out", [P, DB, D]), ("wq", [P, DK, D]), ("dskip", [P, DB]), ("u", [P, DB, CH]), ("gate", [P, DB, CH]))}
    b["weights_loaded"] = ctx.enter_context(nc.semaphore("out_weights"))
    b["ug_loaded"] = [ctx.enter_context(nc.semaphore(n)) for n in ("ug_even", "ug_odd")]
    return b


def load_early(nc, sp, io, scratch, b):
    wl = b["weights_loaded"]
    sp.dma_start(b["w_out"][:], io["WoutT"].rearrange("(k p) n -> p k n", p=P)).then_inc(wl, 16)
    with nc.allow_non_contiguous_dma(reason="512 values once"):
        sp.dma_start(b["dskip"][:], io["D_skip"].rearrange("(k p) -> p k", p=P)).then_inc(wl, 16)
    sp.dma_start(b["wq"][:], io["WqT"].rearrange("(k p) n -> p k n", p=P)).then_inc(wl, 16)
    sp.dma_start(b["u"][:], scratch["ud"][0]).then_inc(b["ug_loaded"][0], 16)
    sp.dma_start(b["gate"][:], scratch["gd"][0]).then_inc(b["ug_loaded"][0], 16)


def load_keys(eng, io, keep, scratch, g):
    Kg, k_ld = keep["Kg"][g], keep["keys_loaded"][g]
    for j, part in enumerate(KPART):
        src = scratch["kd"][part, g * HG * HD:(g + 1) * HG * HD, :]
        eng.dma_start(Kg[j * HD:(j + 1) * HD], src.rearrange("(h e) n -> e h n", h=HG)).then_inc(k_ld, 16)
    eng.dma_start(Kg[ONES0:ROWS_A], scratch["kbd"][:, g * HG:(g + 1) * HG, :]).then_inc(k_ld, 16)
    eng.dma_start(Kg[ROWS_A:ROWS_B], io["ones"]).then_inc(k_ld, 16)


def ssm_output(nc, io, keep, early, scratch):
    with ExitStack() as ctx:
        sb = lambda n, s, t=F32: ctx.enter_context(nc.sbuf_tensor(n, s, t))
        sem = lambda n: ctx.enter_context(nc.semaphore(n))
        ps = [ctx.enter_context(nc.psum_tensor(f"out_ps{i}", [P, 512], F32)) for i in range(8)]
        w_out, wq, dskip, wl, ld = (early[n] for n in ("w_out", "wq", "dskip", "weights_loaded", "ug_loaded"))
        x = sb("x_res", [P, 2, LT, D])
        u = [early["u"], sb("u_odd", [P, DB, CH])]
        gate = [early["gate"], sb("gate_odd", [P, DB, CH])]
        yg = sb("yg", [P, 2, DB, CH])
        r1 = sb("r1", [P, 2, LT, D])
        x1 = sb("x1", [P, 2, LT, D])
        x1T = sb("x1T", [P, DK, CH])
        qs = sb("qs", [P, DK, CH])
        qrest = sb("qrest", [P, DK, CH])
        qpart = sb("qpart", [P, DK, 3, CH], BF16)
        ones = sb("ones3", [P, 1])
        st = [sem("x1q_even"), sem("x1q_odd")]
        norm = Norm(nc, ctx, "n1")
        names = ("yT_done", "skip_done", "yg_done", "proj_done", "r_done", "x1_done", "x1T_in", "x1T_done", "q_in",
                 "q_out", "q1_done", "qrest_done", "q2_done", "q3_done", "flag_in", "flag_set", "ones_set")
        s = {n: sem(n) for n in names}
        y = keep["y"]

        with nc.Block() as block:
            @block.gpsimd
            def _(pool):
                for v in ld:
                    pool.wait_ge(v, 48 * (NC // 2))
                for g in range(2):
                    load_keys(pool, io, keep, scratch, g)

            @block.sync
            def _(sp):
                def load(c):
                    if c >= 2:
                        sp.wait_ge(s["yg_done"], c - 1)
                        sp.wait_ge(s["r_done"], 2 * (c - 1))
                    if c:
                        sp.dma_start(u[c % 2][:], scratch["ud"][c]).then_inc(ld[c % 2], 16)
                        sp.dma_start(gate[c % 2][:], scratch["gd"][c]).then_inc(ld[c % 2], 16)
                    sp.dma_start(x[:, c % 2], io["x"][c * CH:(c + 1) * CH, :].rearrange(
                        "(t p) n -> p t n", p=P)).then_inc(ld[c % 2], 16)
                def store_q(c):
                    sp.wait_ge(s["q3_done"], DK * (c + 1))
                    for m in range(DK):
                        sp.dma_start(scratch["qd"][:, m * P:(m + 1) * P, c * CH:(c + 1) * CH].rearrange(
                            "j p n -> p j n"), qpart[:, m]).then_inc(st[c % 2], 16)

                load(0)
                load(1)
                for c in range(NC):
                    if c + 2 < NC:
                        load(c + 2)
                    sp.wait_ge(s["x1_done"], LT * (c + 1))
                    sp.dma_start(scratch["x1d"][c * CH:(c + 1) * CH, :].rearrange("(t p) n -> p t n", p=P),
                                 x1[:, c % 2]).then_inc(st[c % 2], 16)
                    if c:
                        store_q(c - 1)
                store_q(NC - 1)
                for v in st:
                    sp.wait_ge(v, 48 * (NC // 2))
                sp.wait_ge(s["flag_set"], 1)

            @block.tensor
            def _(pe):
                def transpose_y(c):
                    for d in range(DB):
                        if c:
                            pe.wait_ge(s["skip_done"], DB * (c - 1) + d + 1)
                        for t in range(LT):
                            mm = pe.transpose(ps[d][:, t * P:(t + 1) * P], y[:, LT * c + t, d * P:(d + 1) * P],
                                              keep["ident"][:])
                        mm.then_inc(s["yT_done"], 1)

                pe.wait_ge(s["ones_set"], 1)
                pe.matmul(ps[7][0:1, 0:1], keep["zeros"][:], ones[:], start=True, stop=True).then_inc(s["flag_in"], 1)
                pe.wait_ge(wl, 48)
                def out_proj(c):
                    pe.wait_ge(s["yg_done"], c + 1)
                    for t in range(LT):
                        if c and t % 2 == 0:
                            pe.wait_ge(s["r_done"], 2 * (c - 1) + t // 2 + 1)
                        for k in range(DB):
                            mm = pe.matmul(ps[4 + t // 2][:, (t % 2) * D:(t % 2 + 1) * D],
                                           yg[:, c % 2, k, t * P:(t + 1) * P], w_out[:, k, :],
                                           start=(k == 0), stop=(k == DB - 1))
                        mm.then_inc(s["proj_done"], 1)

                def q_proj(c):
                    pe.wait_ge(s["x1_done"], LT * (c + 1))
                    if c:
                        pe.wait_ge(s["q_out"], DK * c)
                    else:
                        pe.wait_ge(s["flag_set"], 1)
                    for k in range(DK):
                        for t in range(LT):
                            mm = pe.transpose(ps[6 + k][:, t * P:(t + 1) * P], x1[:, c % 2, t, k * P:(k + 1) * P],
                                              keep["ident"][:])
                        mm.then_inc(s["x1T_in"], 1)
                    pe.wait_ge(s["x1T_done"], DK * (c + 1))
                    for m in range(DK):
                        for k in range(DK):
                            mm = pe.matmul(ps[6 + m][:], wq[:, k, m * P:(m + 1) * P], x1T[:, k, :],
                                           start=(k == 0), stop=(k == DK - 1))
                        mm.then_inc(s["q_in"], 1)

                transpose_y(0)
                out_proj(0)
                transpose_y(1)
                for c in range(NC):
                    if c + 1 < NC:
                        out_proj(c + 1)
                    if c + 2 < NC:
                        transpose_y(c + 2)
                    q_proj(c)

            @block.scalar
            def _(act):
                def first_part(c):
                    for k in range(DK):
                        act.wait_ge(s["x1T_in"], DK * c + k + 1)
                        if c:
                            act.wait_ge(s["q_in"], DK * c)
                        act.copy(x1T[:, k, :], ps[6 + k][:]).then_inc(s["x1T_done"], 1)
                    for m in range(DK):
                        act.wait_ge(s["q_in"], DK * c + m + 1)
                        if c:
                            act.wait_ge(s["qrest_done"], DK * (c - 1) + m + 1)
                        if c and m == 0:
                            act.wait_ge(st[(c - 1) % 2], 48 * ((c - 1) // 2 + 1))
                        act.mul(qs[:, m, :], ps[6 + m][:], float(HD) ** -0.5).then_inc(s["q_out"], 1)
                        act.wait_ge(s["q_out"], DK * c + m + 1)
                        act.copy(qpart[:, m, 0, :], qs[:, m, :]).then_inc(s["q1_done"], 1)

                def second_part(c):
                    for m in range(DK):
                        act.wait_ge(s["qrest_done"], DK * c + m + 1)
                        act.copy(qpart[:, m, 1, :], qrest[:, m, :]).then_inc(s["q2_done"], 1)

                for c in range(NC):
                    norm.scalar(act, c)
                    if c:
                        second_part(c - 1)
                    first_part(c)
                second_part(NC - 1)

            @block.vector
            def _(dve):
                dve.memset(ones[:], 1.0).then_inc(s["ones_set"], 1)
                dve.wait_ge(s["flag_in"], 1)
                dve.tensor_scalar(keep["flag"][:], ps[7][0:1, 0:1], 1.0, None, ALU.min).then_inc(s["flag_set"], 1)
                dve.wait_ge(wl, 48)

                def skip_gate(c):
                    dve.wait_ge(ld[c % 2], 48 * (c // 2 + 1))
                    if c >= 2:
                        dve.wait_ge(s["proj_done"], LT * (c - 1))
                    for d in range(DB):
                        dve.wait_ge(s["yT_done"], DB * c + d + 1)
                        dve.scalar_tensor_tensor(yg[:, c % 2, d, :], u[c % 2][:, d, :], dskip[:, d:d + 1], ps[d][:],
                                                 ALU.mult, ALU.add).then_inc(s["skip_done"], 1)
                    dve.wait_ge(s["skip_done"], DB * (c + 1))
                    dve.tensor_tensor(yg[:, c % 2], yg[:, c % 2], gate[c % 2][:], ALU.mult).then_inc(s["yg_done"], 1)

                def residual(c):
                    if c >= 2:
                        dve.wait_ge(s["x1_done"], LT * (c - 1))
                    for i in range(2):
                        dve.wait_ge(s["proj_done"], LT * c + 2 * (i + 1))
                        dve.tensor_tensor(r1[:, c % 2, 2 * i:2 * i + 2, :],
                                          ps[4 + i][:].rearrange("p (t n) -> p t n", t=2),
                                          x[:, c % 2, 2 * i:2 * i + 2, :], ALU.add).then_inc(s["r_done"], 1)

                def first_norm(c):
                    if c >= 2:
                        dve.wait_ge(st[c % 2], 48 * (c // 2))
                        dve.wait_ge(s["x1T_in"], DK * (c - 1))
                    norm.vector(dve, c, lambda t: r1[:, c % 2, t, :], lambda t: x1[:, c % 2, t, :],
                                (s["r_done"], 2 * (c + 1)), s["x1_done"])

                def split_q(c):
                    for m in range(DK):
                        dve.wait_ge(s["q1_done"], DK * c + m + 1)
                        if c:
                            dve.wait_ge(s["q3_done"], DK * (c - 1) + m + 1)
                        dve.tensor_tensor(qrest[:, m, :], qs[:, m, :], qpart[:, m, 0, :],
                                          ALU.subtract).then_inc(s["qrest_done"], 1)
                    for m in range(DK):
                        dve.wait_ge(s["q2_done"], DK * c + m + 1)
                        dve.tensor_tensor(qpart[:, m, 2, :], qrest[:, m, :], qpart[:, m, 1, :],
                                          ALU.subtract).then_inc(s["q3_done"], 1)

                skip_gate(0)
                residual(0)
                for c in range(NC):
                    if c + 1 < NC:
                        skip_gate(c + 1)
                    first_norm(c)
                    if c:
                        split_q(c - 1)
                    if c + 1 < NC:
                        residual(c + 1)
                split_q(NC - 1)


def tail_buffers(nc, ctx, early):
    flat = {n: early[n][:].rearrange("p d n -> p (d n)") for n in ("w_out", "u", "gate")}
    b = {"sel": flat["w_out"][:, 0:P], "wo": flat["u"][:, 0:G * D].rearrange("p (g n) -> p g n", g=G),
         "den": flat["gate"][0:H, 0:L]}
    for n in ("out_proj_weights", "sums_gathered", "den_step", "reciprocals_in_place", "last_in_place"):
        b[n] = ctx.enter_context(nc.semaphore(n))
    return b


def move_sums(sp, X, b, c, back):
    tokens = slice(c * CH, (c + 1) * CH)
    for h in range(HG):
        row = 2 * HD * h + HD
        rows = X[row:row + 1, :, tokens]
        spread = b["den"][G * h:G * (h + 1), tokens]
        if back:
            sp.dma_start(rows, spread).then_inc(b["reciprocals_in_place" if c < NC - 1 else "last_in_place"], 16)
        else:
            sp.dma_start(spread, rows).then_inc(b["sums_gathered"], 16)


def invert(dve, b, lo, hi, step):
    den = b["den"][:, lo * CH:hi * CH]
    dve.wait_ge(b["sums_gathered"], 16 * HG * hi)
    dve.tensor_scalar(den, den, 1.0, None, ALU.add).then_inc(b["den_step"], 1)
    dve.wait_ge(b["den_step"], step + 1)
    dve.reciprocal(den, den).then_inc(b["den_step"], 1)


def attention(nc, io, keep, tail_b, scratch, X):
    with ExitStack() as ctx:
        sb = lambda n, s, t=F32: ctx.enter_context(nc.sbuf_tensor(n, s, t))
        sem = lambda n: ctx.enter_context(nc.semaphore(n))
        pA = [ctx.enter_context(nc.psum_tensor(f"max_ps{i}", [P, 2, 512], F32)) for i in range(2)]
        pB = [ctx.enter_context(nc.psum_tensor(f"exp_ps{i}", [P, CH], F32)) for i in range(3)]
        pX = ctx.enter_context(nc.psum_tensor("pv_ps", [P, CH], F32))
        Kg, k_ld = keep["Kg"], keep["keys_loaded"]
        Qg = [sb(f"Qg{g}", [ROWS_B, HG, CH], BF16) for g in range(G)]
        PB = 4
        PT = sb("PT", [P, PB, HG, CH])
        NM = HG * LT
        half = sb("half", [P, 2, NM, 2])
        nmax = sb("nmax", [P, 2, NM])
        allm = sb("allm", [P, 2, NM])
        mrest = sb("mrest", [NM, 2, P])
        mpart = sb("mpart", [NM, 2, 3, P], BF16)
        MB = sb("MB", [P, 2 * LT, S2], BF16)
        negI = sb("negI", [P, P], BF16)
        V1 = keep["V1"]
        q_ld = [sem(f"Q{g}_loaded") for g in range(G)]
        m_ld = [sem(f"M{g}_loaded") for g in range(G)]
        names = ("mask_loaded", "q_ones", "a_done", "a_max", "half_step", "mT_done", "mT_read",
                 "m_step", "b_done", "exp_done", "pv_done", "x_out", "neg_loaded",
                 "x_started", "loads_started", "guards_started", "parts_started")
        s = {n: sem(n) for n in names}
        UA = 2 * NM
        UH = UA // 2
        UB = KT * HG
        NB = 3
        TB, TP, TX = 3, PB, 1

        def krows(t):
            return P if t < KT - 1 else KLAST

        with nc.Block() as block:
            def item(qc, g, per):
                return qc * (G * per) + g * per

            @block.sync
            def _(sp):
                def load_q(qc, g):
                    for j, part in enumerate(QPART):
                        src = scratch["qd"][part, g * HG * HD:(g + 1) * HG * HD, bass.ds(qc * CH, CH)]
                        sp.dma_start(Qg[g][j * HD:(j + 1) * HD], src.rearrange("(h e) n -> e h n", h=HG)).then_inc(
                            q_ld[g], 16)

                def load_mask(qc, at):
                    src = scratch["md"][bass.ds(qc * CH, CH), :].rearrange("(t p) n -> p t n", p=P)
                    sp.dma_start(MB[:, bass.ds(at, LT), :], src).then_inc(s["mask_loaded"], 16)

                def load_m(qc, g):
                    wait_alone(sp, s["m_step"], item(qc, g, 4) + 4, s["loads_started"])
                    for j in range(3):
                        sp.dma_start(Qg[g][ROWS_A + j:ROWS_A + j + 1], mpart[:, g % 2, j, :]).then_inc(m_ld[g], 16)

                sp.dma_start(negI[:], io["negI"]).then_inc(s["neg_loaded"], 16)
                load_q(0, 0)
                load_q(0, 1)
                load_mask(0, 0)
                load_m(0, 0)
                load_q(0, 2)
                load_q(0, 3)

                def chunk(qc, last):
                    if not last:
                        at = sp.snap((qc + 1) % 2 * LT)
                        wait_alone(sp, s["mask_loaded"], 16 * (qc + 1), s["loads_started"])
                    for g in range(G):
                        if not last and g == 0:
                            sp.wait_ge(s["b_done"], item(qc, g, UB) + 1)
                        if not (last and g == G - 1):
                            load_m(qc + (g + 1) // G, (g + 1) % G)
                        if not last:
                            if g == 0:
                                load_mask(qc + 1, at)
                            wait_alone(sp, s["b_done"], item(qc, g, UB) + UB, s["loads_started"])
                            load_q(qc + 1, g)

                with sp.Fori(0, NC - 1) as qc:
                    chunk(qc, False)
                chunk(NC - 1, True)

                sp.dma_start(tail_b["sel"], io["sel"]).then_inc(tail_b["out_proj_weights"], 16)
                sp.dma_start(tail_b["wo"], io["WoP"].rearrange("g p n -> p g n")).then_inc(
                    tail_b["out_proj_weights"], 16)
                sp.wait_ge(s["x_out"], G * (NC - 1) + TX)
                for c in range(NC - 1):
                    move_sums(sp, X, tail_b, c, back=False)
                sp.wait_ge(tail_b["den_step"], 2)
                for c in range(NC - 1):
                    move_sums(sp, X, tail_b, c, back=True)

            @block.gpsimd
            def _(pool):
                for g in range(2):
                    pool.wait_ge(q_ld[g], 16 * NPAIR)
                for g in range(2, G):
                    load_keys(pool, io, keep, scratch, g)

                def guard(qc, g):
                    at = item(qc, g, 4)
                    new, all_masked = nmax[:, g % 2, :], allm[:, g % 2, :]
                    wait_alone(pool, s["half_step"], at + 1, s["guards_started"])
                    pool.tensor_scalar(all_masked, new, MASKED / 2, 3e38, ALU.is_gt, ALU.mult).then_inc(
                        s["half_step"], 1)
                    pool.wait_ge(s["half_step"], at + 2)
                    pool.tensor_tensor(all_masked, all_masked, all_masked, ALU.mult).then_inc(s["half_step"], 1)
                    pool.wait_ge(s["half_step"], at + 3)
                    pool.tensor_tensor(new, new, all_masked, ALU.add).then_inc(s["half_step"], 1)

                def parts(qc, g):
                    part, rest, at = mpart[:, g % 2], mrest[:, g % 2, :], item(qc, g, 4)
                    if g >= 2:
                        pool.wait_ge(m_ld[g - 2], qc * 48 + 48)
                    elif not (isinstance(qc, int) and qc == 0):
                        pool.wait_ge(m_ld[g + 2], qc * 48)
                    wait_alone(pool, s["mT_read"], item(qc, g, 1) + 1, s["parts_started"])
                    pool.tensor_copy(part[:, 0, :], rest).then_inc(s["m_step"], 1)
                    pool.wait_ge(s["m_step"], at + 1)
                    pool.tensor_tensor(rest, rest, part[:, 0, :], ALU.subtract).then_inc(s["m_step"], 1)
                    wait_alone(pool, s["m_step"], at + 2, s["parts_started"])
                    pool.tensor_copy(part[:, 1, :], rest).then_inc(s["m_step"], 1)
                    pool.wait_ge(s["m_step"], at + 3)
                    pool.tensor_tensor(part[:, 2, :], rest, part[:, 1, :], ALU.subtract).then_inc(s["m_step"], 1)

                def items(qc):
                    for g in range(G):
                        guard(qc, g)
                        parts(qc, g)

                items(0)
                with pool.Fori(1, NC) as qc:
                    items(qc)

            @block.tensor
            def _(pe):
                def max_unit(qc, g, a, masked):
                    hh, t, hf = a // (2 * LT), a // 2 % LT, a % 2
                    if a == 0:
                        pe.wait_ge(q_ld[g], qc * (16 * NPAIR) + 16 * NPAIR)
                        pe.wait_ge(k_ld[g], 16 * (NPAIR + 2))
                        if masked:
                            pe.wait_ge(s["mask_loaded"], qc * 16 + 16)
                    if not (isinstance(qc, int) and qc == 0 and g == 0 and a < 2):
                        pe.wait_ge(s["a_max"], item(qc, g, UA) + a - 1)
                    for j in range(2):
                        lo = MSTEP * (2 * hf + j)
                        out = pA[a % 2][:, j, 0:MW]
                        mm = pe.matmul(out, Qg[g][0:ROWS_A, hh, t * P:(t + 1) * P], Kg[g][0:ROWS_A, hh, lo:lo + MW],
                                       start=True, stop=not masked)
                        if masked:
                            mm = pe.matmul(out, negI[:], MB[:, bass.ds((qc % 2) * LT + t, 1), lo:lo + MW],
                                           start=False, stop=True)
                    mm.then_inc(s["a_done"], 1)

                def max_rows(qc, g, user=None):
                    if user:
                        pe.wait_ge(s["a_max"], item(user[0], user[1], UA) + user[2] + 1)
                    pe.wait_ge(s["half_step"], item(qc, g, 4) + 4)
                    pe.transpose(pA[0][0:NM, 0, 0:P], nmax[:, g % 2, :], keep["ident"][:]).then_inc(s["mT_done"], 1)

                def exp_unit(qc, g, t, hh, masked):
                    b = t * HG + hh
                    if b == 0:
                        pe.wait_ge(m_ld[g], qc * 48 + 48)
                    i = UB * g + b
                    back = NB if i >= NB else {0: 1, 1: 3, 2: 2}[i]
                    pe.wait_ge(s["exp_done"], item(qc, g, UB) + b - back + 1 + TB)
                    out = pB[i % NB][0:krows(t)]
                    mm = pe.matmul(out, Kg[g][:, hh, t * P:t * P + krows(t)], Qg[g][:, hh, :],
                                   start=True, stop=not masked)
                    if masked:
                        for qt in range(LT):
                            mm = pe.matmul(out[:, qt * P:(qt + 1) * P],
                                           MB[:, bass.ds((qc % 2) * LT + qt, 1), t * P:t * P + krows(t)], negI[:],
                                           start=False, stop=(qt == LT - 1))
                    mm.then_inc(s["b_done"], 1)

                def values(qc, g, t):
                    pe.wait_ge(s["exp_done"], item(qc, g, UB) + HG * (t + 1) + TB)
                    if t == 0:
                        pe.wait_ge(s["x_out"], item(qc, g, 1) + TX)
                    for hh in range(HG):
                        mm = pe.matmul(pX[2 * HD * hh:2 * HD * (hh + 1), :],
                                       V1[0:krows(t), t, g * HG + hh, :],
                                       PT[0:krows(t), (KT * g + t) % PB, hh, :],
                                       start=(t == 0), stop=(t == KT - 1), skip_group_check=True)
                    mm.then_inc(s["pv_done"], 1)

                def chunk(qc, last, masked):
                    nc.disable_value_cache = masked
                    for g in range(G):
                        run(qc, g, last, masked)
                    nc.disable_value_cache = False

                def run(qc, g, last, masked):
                    after = [(qc + (g + i) // G, (g + i) % G) for i in (1, 2)]
                    k = 0
                    rows_taken = False
                    until = UA if not last or g < G - 2 else UH if g == G - 2 else 0
                    for t in range(KT):
                        hh = 0
                        for step in "EEMVEMEM":
                            if step == "E":
                                exp_unit(qc, g, t, hh, masked)
                                hh += 1
                                if k == UH + 4 and not rows_taken:
                                    max_rows(*after[0], (*after[1], 2))
                                    rows_taken = True
                            elif step == "M" and k < min(until, (t + 1) * UA // KT):
                                if k == UH + 4:
                                    assert rows_taken
                                    pe.wait_ge(s["mT_read"], item(qc, g, 1) + 2)
                                max_unit(*after[k // UH], (k + UH) % UA, masked)
                                k += 1
                            elif step == "V" and t >= 2:
                                values(qc, g, t - 2)
                            elif step == "V" and g > 0:
                                values(qc, g - 1, KT - 2 + t)
                        if until == UH and t == KT - 4:
                            max_rows(*after[0])
                    assert k == until
                    if g == G - 1:
                        for t in (KT - 2, KT - 1):
                            values(qc, g, t)

                def start(masked):
                    for a in range(UA):
                        max_unit(0, 0, a, masked)
                    for a in range(4):
                        max_unit(0, 1, a, masked)
                    max_rows(0, 0, (0, 1, 2))
                    pe.wait_ge(s["mT_read"], 1)
                    for a in range(4, UH):
                        max_unit(0, 1, a, masked)

                pe.wait_ge(s["neg_loaded"], 16)
                pe.wait_ge(s["q_ones"], 16 * G)
                zeros = pe.value_load(keep["flag"][0:1, 0:1], min_val=0, max_val=1)
                with pe.If(zeros > 0):
                    start(True)
                with pe.Else():
                    start(False)
                with pe.Fori(0, NC - 1) as qc:
                    with pe.If(zeros > 0):
                        chunk(qc, False, True)
                    with pe.Else():
                        chunk(qc, False, False)
                with pe.If(zeros > 0):
                    chunk(NC - 1, True, True)
                with pe.Else():
                    chunk(NC - 1, True, False)

            @block.scalar
            def _(act):
                for g in range(G):
                    act.dma_start(Qg[g][ONES0:ROWS_A], io["ones"][:, 0:HG, 0:CH]).then_inc(s["q_ones"], 16)
                act.sem_inc(s["exp_done"], TB)

                def x_from_psum(qc, g):
                    wait_alone(act, s["pv_done"], item(qc, g, KT) + KT + TP, s["x_started"])
                    act.copy(X[:, g, bass.ds(qc * CH, CH)], pX[:]).then_inc(s["x_out"], 1)

                def run(qc, g):
                    for t in range(KT):
                        for hh in range(HG):
                            b = t * HG + hh
                            act.wait_ge(s["b_done"], item(qc, g, UB) + b + 1)
                            if hh == 0:
                                act.wait_ge(s["pv_done"], item(qc, g, KT) + t - PB + 1 + TP)
                            act.activation(PT[0:krows(t), (KT * g + t) % PB, hh, :], pB[(UB * g + b) % NB][0:krows(t)],
                                           ACT.Exp).then_inc(s["exp_done"], 1)
                            if t == 1 and hh == 2 and g > 0:
                                x_from_psum(qc, g - 1)
                    if g == G - 1:
                        x_from_psum(qc, g)

                with act.Fori(0, NC) as qc:
                    for g in range(G):
                        run(qc, g)

            @block.vector
            def _(dve):
                dve.sem_inc(s["x_out"], TX)
                dve.sem_inc(s["pv_done"], TP)

                def maxima(qc, g, lo, hi):
                    for a in range(lo, hi):
                        dve.wait_ge(s["a_done"], item(qc, g, UA) + a + 1)
                        if a == 0 and not (isinstance(qc, int) and qc == 0 and g < 2):
                            dve.wait_ge(s["half_step"], item(qc, g, 4) - 4)
                        dve.tensor_reduce(half[:, g % 2, a // 2, a % 2:a % 2 + 1], pA[a % 2][:, :, 0:MW], AX.XY,
                                          ALU.max, negate=True).then_inc(s["a_max"], 1)

                def both(qc, g):
                    dve.wait_ge(s["a_max"], item(qc, g, UA) + UA)
                    if not (isinstance(qc, int) and qc == 0 and g < 2):
                        dve.wait_ge(s["mT_done"], item(qc, g, 1) - 1)
                    dve.tensor_reduce(nmax[:, g % 2, :], half[:, g % 2], AX.X, ALU.min).then_inc(s["half_step"], 1)

                def rows_out(qc, g):
                    dve.wait_ge(s["mT_done"], item(qc, g, 1) + 1)
                    if not (isinstance(qc, int) and qc == 0 and g < 2):
                        dve.wait_ge(s["m_step"], item(qc, g, 4) - 4)
                    dve.tensor_copy(mrest[:, g % 2, :], pA[0][0:NM, 0, 0:P]).then_inc(s["mT_read"], 1)

                def run(qc, g, last):
                    after = [(qc + (g + i) // G, (g + i) % G) for i in (1, 2)]
                    if last and g == G - 1:
                        return
                    maxima(*after[0], UH, UA)
                    both(*after[0])
                    if last and g == G - 2:
                        rows_out(*after[0])
                        return
                    maxima(*after[1], 0, 4)
                    rows_out(*after[0])
                    maxima(*after[1], 4, UH)

                maxima(0, 0, 0, UA)
                both(0, 0)
                maxima(0, 1, 0, 4)
                rows_out(0, 0)
                maxima(0, 1, 4, UH)
                with dve.Fori(0, NC - 1) as qc:
                    for g in range(G):
                        run(qc, g, False)
                for g in range(G):
                    run(NC - 1, g, True)
                invert(dve, tail_b, 0, NC - 1, 0)


def tail(nc, io, keep, tail_b, scratch, X, out):
    with ExitStack() as ctx:
        sb = lambda n, s, t=F32: ctx.enter_context(nc.sbuf_tensor(n, s, t))
        sem = lambda n: ctx.enter_context(nc.semaphore(n))
        ps = [ctx.enter_context(nc.psum_tensor(f"t_ps{i}", [P, 512], F32)) for i in range(8)]
        sel, wo, wl_o, rec_ld = (tail_b[n] for n in ("sel", "wo", "out_proj_weights", "reciprocals_in_place"))
        gates = ("f", "i", "c")
        w = {g: sb(f"ffn_w{g}", [P, DK, D]) for g in (*gates, "o")}
        uw = {g: sb(f"ffn_u{g}", [P, DK, D]) for g in (*gates, "o")}
        gb = sb("gb", [P, 3, DK])
        bo = sb("bo", [1, D])
        onerow = sb("onerow", [1, P])
        c0 = sb("c0", [P, DK])
        x1 = sb("x1r", [P, 2, LT, D])
        on = sb("on", [P, G, CH])
        r2 = sb("r2", [P, LT, D])
        x2 = sb("x2", [P, 2, LT, D])
        x2T = sb("x2T", [P, DK, CH])
        act_g = {g: sb(f"act_{g}", [P, DK, CH]) for g in gates}
        ig = sb("ig", [P, DK, CH])
        cs = sb("cs", [P, DK, CH])
        hh = sb("hh", [P, LT, D])
        res = sb("res", [P, 2, LT, D])
        wl = sem("gate_weights")
        ld = [sem("x1_even"), sem("x1_odd")]
        st = [sem("out_even"), sem("out_odd")]
        norm2, norm3 = Norm(nc, ctx, "n2"), Norm(nc, ctx, "n3")
        names = ("row_set", "gb_in", "gb_set", "sum_done", "on_done", "proj_done", "r_done", "x2_done",
                 "x2T_in", "x2T_done", "gate_in", "gate_done", "ig_done", "c_done", "h_in", "h_done", "r3_done",
                 "res_done")
        s = {n: sem("t_" + n) for n in names}
        NW = 1 + 2 * 4 + 3 + 1
        NG = 3 * DK

        with nc.Block() as block:
            @block.sync
            def _(sp):
                def load(c):
                    if c >= 2:
                        sp.wait_ge(s["r_done"], 2 * (c - 1))
                    sp.dma_start(x1[:, c % 2], scratch["x1d"][c * CH:(c + 1) * CH, :].rearrange(
                        "(t p) n -> p t n", p=P)).then_inc(ld[c % 2], 16)

                load(0)
                move_sums(sp, X, tail_b, NC - 1, back=False)
                sp.dma_start(bo[:], io["bo"]).then_inc(wl, 16)
                for g in (*gates, "o"):
                    sp.dma_start(w[g][:], io[f"w{g}T"].rearrange("(k p) n -> p k n", p=P)).then_inc(wl, 16)
                    sp.dma_start(uw[g][:], io[f"u{g}T"].rearrange("(k p) n -> p k n", p=P)).then_inc(wl, 16)
                with nc.allow_non_contiguous_dma(reason="256 values once"):
                    for j, g in enumerate(gates):
                        sp.dma_start(gb[:, j, :], io[f"b{g}"].rearrange("(k p) -> p k", p=P)).then_inc(wl, 16)
                    sp.dma_start(c0[:], io["in_c"].rearrange("(k p) -> p k", p=P)).then_inc(wl, 16)

                sp.wait_ge(tail_b["den_step"], 4)
                move_sums(sp, X, tail_b, NC - 1, back=True)
                load(1)
                for c in range(NC):
                    if c >= 1 and c + 1 < NC:
                        load(c + 1)
                    sp.wait_ge(s["res_done"], LT * (c + 1))
                    sp.dma_start(out[c * CH:(c + 1) * CH, :].rearrange("(t p) n -> p t n", p=P),
                                 res[:, c % 2]).then_inc(st[c % 2], 16)
                for v in st:
                    sp.wait_ge(v, 16 * (NC // 2))

            @block.gpsimd
            def _(pool):
                pool.memset(onerow[:], 1.0).then_inc(s["row_set"], 1)

            @block.tensor
            def _(pe):
                def state_bias():
                    pe.wait_ge(wl, 16 * NW)
                    for j, g in enumerate(gates):
                        for m in range(DK):
                            for k in range(DK):
                                mm = pe.matmul(ps[6][:, j * DK + m:j * DK + m + 1], uw[g][:, k, m * P:(m + 1) * P],
                                               c0[:, k:k + 1], start=(k == 0), stop=(k == DK - 1))
                    mm.then_inc(s["gb_in"], 1)

                def sums(c):
                    if c < NC - 1:
                        pe.wait_ge(rec_ld, 16 * HG * (NC - 1))
                    else:
                        pe.wait_ge(tail_b["last_in_place"], 16 * HG)
                    for g in range(G):
                        j = G * c + g
                        if j >= 2:
                            pe.wait_ge(s["on_done"], j - 1)
                        pe.matmul(ps[j % 2][:], sel, X[:, g, c * CH:(c + 1) * CH], start=True,
                                  stop=True).then_inc(s["sum_done"], 1)

                def out_proj(c):
                    pe.wait_ge(s["on_done"], G * (c + 1))
                    for t in range(LT):
                        if c and t % 2 == 0:
                            pe.wait_ge(s["r_done"], 2 * (c - 1) + t // 2 + 1)
                        for g in range(G):
                            mm = pe.matmul(ps[2 + t // 2][:, (t % 2) * D:(t % 2 + 1) * D],
                                           on[:, g, t * P:(t + 1) * P], wo[:, g, :], start=(g == 0),
                                           stop=(g == G - 1))
                        mm.then_inc(s["proj_done"], 1)

                def gate_products(c):
                    pe.wait_ge(s["x2_done"], LT * (c + 1))
                    if c:
                        pe.wait_ge(s["h_done"], 2 * c)
                    for k in range(DK):
                        for t in range(LT):
                            mm = pe.transpose(ps[4 + k][:, t * P:(t + 1) * P], x2[:, c % 2, t, k * P:(k + 1) * P],
                                              keep["ident"][:])
                        mm.then_inc(s["x2T_in"], 1)
                    pe.wait_ge(s["x2T_done"], DK * (c + 1))
                    for j, g in enumerate(gates):
                        for m in range(DK):
                            r = NG * c + DK * j + m
                            if r >= 2:
                                pe.wait_ge(s["gate_done"], r - 1)
                            elif r == 0:
                                pe.wait_ge(s["gb_set"], 1)
                            for k in range(DK):
                                mm = pe.matmul(ps[6 + r % 2][:], w[g][:, k, m * P:(m + 1) * P], x2T[:, k, :],
                                               start=(k == 0), stop=(k == DK - 1))
                            mm.then_inc(s["gate_in"], 1)

                def h_products(c):
                    for t in range(LT):
                        o = ps[4 + t // 2][:, (t % 2) * D:(t % 2 + 1) * D]
                        for k in range(DK):
                            pe.matmul(o, x2T[:, k, t * P:(t + 1) * P], w["o"][:, k, :], start=(k == 0), stop=False)
                        if t == 0:
                            pe.wait_ge(s["c_done"], c + 1)
                        for k in range(DK):
                            pe.matmul(o, cs[:, k, t * P:(t + 1) * P], uw["o"][:, k, :], start=False, stop=False)
                        pe.matmul(o, onerow[:], bo[:], start=False, stop=True).then_inc(s["h_in"], 1)

                pe.wait_ge(s["row_set"], 1)
                pe.wait_ge(wl_o, 32)
                sums(0)
                out_proj(0)
                sums(1)
                state_bias()
                for c in range(NC):
                    gate_products(c)
                    if c + 1 < NC:
                        out_proj(c + 1)
                    h_products(c)
                    if c + 2 < NC:
                        sums(c + 2)

            @block.scalar
            def _(act):
                norm2.scalar(act, 0)
                for c in range(NC):
                    for k in range(DK):
                        act.wait_ge(s["x2T_in"], DK * c + k + 1)
                        if c:
                            act.wait_ge(s["h_in"], LT * c)
                        act.copy(x2T[:, k, :], ps[4 + k][:]).then_inc(s["x2T_done"], 1)
                    if c:
                        norm3.scalar(act, c - 1)
                        act.wait_ge(s["c_done"], c)
                    else:
                        act.wait_ge(s["gb_set"], 1)
                    for j, g in enumerate(gates):
                        for m in range(DK):
                            r = NG * c + DK * j + m
                            act.wait_ge(s["gate_in"], r + 1)
                            act.activation(act_g[g][:, m, :], ps[6 + r % 2][:], ACT.Tanh if g == "c" else ACT.Sigmoid,
                                           bias=gb[:, j, m:m + 1]).then_inc(s["gate_done"], 1)
                    if c + 1 < NC:
                        norm2.scalar(act, c + 1)
                    for i in range(2):
                        act.wait_ge(s["h_in"], LT * c + 2 * (i + 1))
                        if c:
                            act.wait_ge(s["res_done"], LT * c)
                        act.activation(hh[:, 2 * i:2 * i + 2, :], ps[4 + i][:].rearrange("p (t n) -> p t n", t=2),
                                       ACT.Tanh).then_inc(s["h_done"], 1)
                norm3.scalar(act, NC - 1)

            @block.vector
            def _(dve):
                def divide(c):
                    if c < NC - 1:
                        dve.wait_ge(rec_ld, 16 * HG * (NC - 1))
                    else:
                        dve.wait_ge(tail_b["last_in_place"], 16 * HG)
                    if c:
                        dve.wait_ge(s["proj_done"], LT * c)
                    for g in range(G):
                        j = G * c + g
                        dve.wait_ge(s["sum_done"], j + 1)
                        dve.tensor_tensor(on[:, g, :], X[:, g, c * CH:(c + 1) * CH], ps[j % 2][:],
                                          ALU.mult).then_inc(s["on_done"], 1)

                def second_norm(c):
                    dve.wait_ge(ld[c % 2], 16 * (c // 2 + 1))
                    if c:
                        dve.wait_ge(s["x2_done"], LT * c)
                    for i in range(2):
                        dve.wait_ge(s["proj_done"], LT * c + 2 * (i + 1))
                        dve.tensor_tensor(r2[:, 2 * i:2 * i + 2, :],
                                          ps[2 + i][:].rearrange("p (t n) -> p t n", t=2),
                                          x1[:, c % 2, 2 * i:2 * i + 2, :], ALU.add).then_inc(s["r_done"], 1)
                    if c >= 2:
                        dve.wait_ge(s["r3_done"], c - 1)
                    norm2.vector(dve, c, lambda t: r2[:, t, :], lambda t: x2[:, c % 2, t, :],
                                 (s["r_done"], 2 * (c + 1)), s["x2_done"])

                def cell(c):
                    dve.wait_ge(s["gate_done"], NG * (c + 1))
                    if c:
                        dve.wait_ge(s["h_in"], LT * c)
                    dve.tensor_tensor(ig[:], act_g["i"][:], act_g["c"][:], ALU.mult).then_inc(s["ig_done"], 1)
                    dve.wait_ge(s["ig_done"], c + 1)
                    for m in range(DK):
                        last = dve.scalar_tensor_tensor(cs[:, m, :], act_g["f"][:, m, :], c0[:, m:m + 1], ig[:, m, :],
                                                        ALU.mult, ALU.add)
                    last.then_inc(s["c_done"], 1)

                def third_norm(c):
                    dve.wait_ge(s["h_done"], 2 * (c + 1))
                    dve.tensor_tensor(hh[:], hh[:], x2[:, c % 2], ALU.add).then_inc(s["r3_done"], 1)
                    if c >= 2:
                        dve.wait_ge(st[c % 2], 16 * (c // 2))
                    norm3.vector(dve, c, lambda t: hh[:, t, :], lambda t: res[:, c % 2, t, :],
                                 (s["r3_done"], c + 1), s["res_done"])

                divide(0)
                second_norm(0)
                divide(1)
                dve.wait_ge(wl, 16 * NW)
                dve.wait_ge(s["gb_in"], 1)
                dve.tensor_tensor(gb[:], gb[:], ps[6][:, 0:NG].rearrange("p (j m) -> p j m", j=3),
                                  ALU.add).then_inc(s["gb_set"], 1)
                invert(dve, tail_b, NC - 1, NC, 2)
                for c in range(NC):
                    cell(c)
                    if c + 1 < NC:
                        second_norm(c + 1)
                    if c + 2 < NC:
                        divide(c + 2)
                    third_norm(c)


def program(nc, io, out):
    scratch = {}
    for name, shape, t in (("kd", [3, D, S2], BF16), ("kbd", [3, H, S2], BF16), ("qd", [3, D, L], BF16),
                           ("md", [L, S2], BF16), ("ud", [NC, P, DB, CH], F32), ("gd", [NC, P, DB, CH], F32),
                           ("x1d", [L, D], F32)):
        scratch[name] = nc.dram_tensor("scratch_" + name, shape, t, kind="Internal").ap()
    with ExitStack() as ctx:
        keep = {
            "ident": ctx.enter_context(nc.sbuf_tensor("ident", [P, P], F32)),
            "V1": ctx.enter_context(nc.sbuf_tensor("V1", [P, KT, H, 2 * HD], F32)),
            "zeros": ctx.enter_context(nc.sbuf_tensor("zeros", [P, 1], F32)),
            "flag": ctx.enter_context(nc.sbuf_tensor("flag", [1, 1], I32)),
        }
        y = ctx.enter_context(nc.sbuf_tensor("y_or_X", [P, L // P, DI], F32))
        X = y[:].rearrange("p t n -> p (t n)").rearrange("p (g n) -> p g n", g=G)
        keep["y"] = y
        early = early_buffers(nc, ctx)
        with ExitStack() as ssm_ctx:
            ssm = {n: ssm_ctx.enter_context(nc.sbuf_tensor(n, shape, F32)) for n, shape in (
                ("delta", [P, DB, L]), ("duT", [P, L // P, DI]), ("bc", [P, L // P, R + 2 * NS]),
                ("A", [P, DB, NS]))}
            with ExitStack() as in_ctx:
                inputs = input_buffers(nc, in_ctx, ssm["duT"])
                keys_values(nc, io, keep, inputs, ssm["delta"], scratch)
                ssm_inputs(nc, io, keep, inputs, ssm, scratch)
            ssm_scan(nc, io, keep, ssm, early, scratch)
        with ExitStack() as key_ctx:
            keep["Kg"] = [key_ctx.enter_context(nc.sbuf_tensor(f"Kg{g}", [ROWS_B, HG, S2], BF16)) for g in range(G)]
            keep["keys_loaded"] = [key_ctx.enter_context(nc.semaphore(f"K{g}_loaded")) for g in range(G)]
            ssm_output(nc, io, keep, early, scratch)
            tail_b = tail_buffers(nc, ctx, early)
            attention(nc, io, keep, tail_b, scratch, X)
        tail(nc, io, keep, tail_b, scratch, X, out)


def kernel(**inputs):
    import numpy as np
    import ml_dtypes
    import concourse.bacc as bacc
    from concourse.bass_utils import run_bass_kernel_spmd as launch

    g = {k: np.asarray(v) for k, v in inputs.items()}
    wo_rows = np.zeros((G, P, D), np.float32)
    woT = g["L0_xattn_W_o"].T
    for h in range(H):
        wo_rows[h // HG, 2 * HD * (h % HG):2 * HD * (h % HG) + HD] = woT[h * HD:(h + 1) * HD]
    sel = np.zeros((P, P), np.float32)
    for h in range(HG):
        sel[2 * HD * h + HD, 2 * HD * h:2 * HD * h + HD] = 1.0
    ratio = 2.0 ** (-8.0 / H)
    arrays = {
        "x": g["x"][0], "xT": g["x"][0].T, "ctxT": g["ctx_1024"][0].T, "kpos": g["itok_BxS2_1_8191"],
        "mask": g["mask_BxSxS2_if1"][0],
        "WinT": g["L0_attn_W_in"].T, "conv_w": g["L0_attn_conv_w"], "conv_b": g["L0_attn_conv_b"],
        "WxT": g["L0_attn_W_x"].T, "WdtT": g["L0_attn_W_dt"].T, "dt_bias": g["L0_attn_dt_bias"],
        "A_log": g["L0_attn_A_log"], "D_skip": g["L0_attn_D_skip"], "WoutT": g["L0_attn_W_out"].T,
        "WqT": g["L0_xattn_W_q"].T, "WkT": g["L0_xattn_W_k"].T, "WvT": g["L0_xattn_W_v"].T, "WoP": wo_rows,
        "bo": g["L0_ffn_bo"][None], "in_c": g["L0_ffn_in_c"],
        "ident": np.eye(P, dtype=np.float32), "sel": sel,
        "negI": (-MASKED * np.eye(P, dtype=np.float32)).astype(ml_dtypes.bfloat16),
        "ones": np.ones((3, HG, S2), ml_dtypes.bfloat16),
        "slopes": np.array([[ratio ** i] for i in range(1, H + 1)], np.float32),
    }
    for n in "fico":
        arrays[f"w{n}T"] = g[f"L0_ffn_w{n}"].T
        arrays[f"u{n}T"] = g[f"L0_ffn_u{n}"].T
        if n != "o":
            arrays[f"b{n}"] = g[f"L0_ffn_b{n}"]
    arrays = {k: np.ascontiguousarray(v) for k, v in arrays.items()}
    nc = bacc.Bacc("TRN2", target_bir_lowering=False, num_devices=1)
    io = {k: nc.dram_tensor("in_" + k, v.shape, mybir.dt.from_np(v.dtype), kind="ExternalInput").ap()
          for k, v in arrays.items()}
    out = nc.dram_tensor("out", [L, D], F32, kind="ExternalOutput").ap()
    program(nc, io, out)
    r = launch(nc, [{"in_" + k: v for k, v in arrays.items()}], core_ids=[0])
    return r.results[0]["out"].reshape(1, L, D)
```
